# Optimizing a Trainium2 kernel written in Bass

```python
import numpy as np
import jax
import jax.numpy as jnp

def _softmax(x, axis=-1):
    return jax.nn.softmax(x, axis=axis)
def _gelu(x):
    return jax.nn.gelu(x, approximate=True)
def _silu(x):
    return jax.nn.silu(x)
def _sigmoid(x):
    return jax.nn.sigmoid(x)
def _layernorm(x, axis=-1, eps=1e-5):
    m = jnp.mean(x, axis=axis, keepdims=True)
    v = jnp.var(x, axis=axis, keepdims=True)
    return (x - m) / jnp.sqrt(v + eps)
def _scatter_add(tgt, idx, src, axis=0):
    return tgt.at[idx].add(src)
def _segment_sum(src, seg, n):
    return jax.ops.segment_sum(src, seg, n)

kernel_name = 'mk_adj_preln_d1_adj_256_335a5b'

def setup_inputs(seed: int = 0):
    np.random.seed(seed)
    _w = jnp.asarray
    def _rec_inputs():
        import jax
        import jax.numpy as jnp
        _gk = jax.random.key(seed)
        x = -0.000929 + 1 * jax.random.normal(jax.random.fold_in(_gk, 1), (8192, 256), jnp.float32)
        _a = jax.random.bernoulli(jax.random.fold_in(_gk, 2), 0.00390625, (8192, 8192))
        _a = jnp.logical_or(_a, jnp.eye(8192, dtype=bool))
        _af = _a.astype(jnp.float32)
        _af = _af * jax.random.uniform(jax.random.fold_in(_gk, 3), (8192, 8192), jnp.float32, 0.05, 1)
        adj = _af
        return x, adj
    x, adj = _rec_inputs()
    def _L0_gnn_setup():
        import jax, jax.numpy as jnp
        import numpy as np
        N = 4096
        IN = 256
        H = 8
        D = 32
        ALPHA = 0.2
        key = jax.random.key(seed)
        ks = jax.random.split(key, 9)
        xav = lambda k, sh: jax.random.normal(k, sh, jnp.float32) * np.float32(np.sqrt(2.0 / (sh[0] + sh[-1])))
        return {'x': jax.random.normal(ks[0], (N, IN), jnp.float32), 'adj_matrix': jax.random.uniform(ks[1], (N, N), jnp.float32), 'W': xav(ks[2], (H * D, IN)), 'We': xav(ks[3], (H, 1)), 'be': jnp.zeros((H,), jnp.float32), 'a_src': xav(ks[4], (H, D)), 'a_dst': xav(ks[5], (H, D)), 'Wr': xav(ks[6], (H * D, IN)), 'br': jnp.zeros((H * D,), jnp.float32)}
    _L0_gnn_all = _L0_gnn_setup()
    _L0_gnn_in = {k: v for k, v in _L0_gnn_all.items() if k in ('W', 'We', 'be', 'a_src', 'a_dst', 'Wr', 'br', )}
    del _L0_gnn_all

    return {
        "x": x,
        "adj": adj,
        "L0_gnn_W": _L0_gnn_in["W"],
        "L0_gnn_We": _L0_gnn_in["We"],
        "L0_gnn_be": _L0_gnn_in["be"],
        "L0_gnn_a_src": _L0_gnn_in["a_src"],
        "L0_gnn_a_dst": _L0_gnn_in["a_dst"],
        "L0_gnn_Wr": _L0_gnn_in["Wr"],
        "L0_gnn_br": _L0_gnn_in["br"],
    }

def reference(x, adj, L0_gnn_W, L0_gnn_We, L0_gnn_be, L0_gnn_a_src, L0_gnn_a_dst, L0_gnn_Wr, L0_gnn_br):
    import jax
    import jax.numpy as jnp
    def _L0_gnn_ref(x, adj_matrix, W, We, be, a_src, a_dst, Wr, br):
        import jax, jax.numpy as jnp
        import numpy as np
        N = 4096
        IN = 256
        H = 8
        D = 32
        ALPHA = 0.2
        n = x.shape[0]
        h = (x @ W.T).reshape(n, H, D)
        s_src = jnp.einsum('nhd,hd->nh', h, a_src)
        s_dst = jnp.einsum('nhd,hd->nh', h, a_dst)
        attn = s_src[:, None, :] + s_dst[None, :, :]
        attn = attn + adj_matrix[:, :, None] * We[:, 0] + be
        mask = (adj_matrix > 0)[:, :, None]
        attn = jnp.where(mask, attn, -jnp.inf)
        attn = jax.nn.leaky_relu(attn, ALPHA)
        attn = jax.nn.softmax(attn, axis=1)
        h_out = jnp.einsum('ijh,jhd->ihd', attn, h).reshape(n, H * D)
        return h_out + x @ Wr.T + br

    h = jnp.maximum(_layernorm(x, axis=-1), 0.0)
    x = x + _L0_gnn_ref(h, adj, L0_gnn_W, L0_gnn_We, L0_gnn_be, L0_gnn_a_src, L0_gnn_a_dst, L0_gnn_Wr, L0_gnn_br)
    return x


_drawn_inputs = setup_inputs


def setup_inputs(seed=0):
    import zlib

    import numpy as np

    out = dict(_drawn_inputs(seed))
    spreads = {'L0_gnn_be': (0.0, 0.8), 'L0_gnn_br': (0.0, 0.1)}
    factors = {'L0_gnn_We': 3.947, 'L0_gnn_a_src': 2.776}
    for name, (base, spread) in spreads.items():
        noise = np.random.default_rng([zlib.crc32(name.encode()), seed]).standard_normal(out[name].shape)
        drawn = base * np.exp(spread * noise) if base else spread * noise
        out[name] = jnp.asarray(drawn.astype(out[name].dtype))
    for name, factor in factors.items():
        out[name] = (out[name] * factor).astype(out[name].dtype)
    return out
```

```python
import concourse.bass as bass
from concourse import mybir
from contextlib import ExitStack

F32 = mybir.dt.float32
BF16 = mybir.dt.bfloat16
U32 = mybir.dt.uint32
I32 = mybir.dt.int32
ALU = mybir.AluOpType
ACT = mybir.ActivationFunctionType
AX = mybir.AxisListType

P = 128
ALPHA = 0.2
EPS = 1e-5
SEG = 256
SLOTS = 64
GS = 8
NG = SLOTS // GS
FIRM = 5
CODE = 8192
PAD = -3.0e38
FLOOR = -5.0e37
CHUNK = 64
MAIN, SLOW = 0, 1


def build(nc, x, adj, W, We, be, a_src, a_dst, Wr, br, out):
    N, IN = x.shape
    H, D = a_src.shape
    E = D + 1
    C = H * E
    RS = IN + H
    T = N // P
    NSEG = N // SEG
    KC = IN // P
    HC = H // KC
    XQ = 4
    CNT = 2048
    NCNT = N // CNT
    NCH = N // CHUNK

    h_rows = nc.dram_tensor("h_rows", (N, C), F32, kind="Internal").ap()
    r_rows = nc.dram_tensor("r_rows", (N, IN), F32, kind="Internal").ap()

    ctx = ExitStack()
    with ctx:
        def sb(name, shape, dt=F32):
            return ctx.enter_context(nc.sbuf_tensor(name, shape, dt))

        def ps(name, shape):
            return ctx.enter_context(nc.psum_tensor(name, shape, F32))

        def sem(name):
            return ctx.enter_context(nc.semaphore(name))

        ident = sb("ident", [P, P])
        ones = sb("ones", [1, P])
        w_nat = sb("w_nat", [P, KC, IN])
        wr_nat = sb("wr_nat", [P, KC, IN])
        w_t = sb("w_t", [P, KC, C])
        wr_t = sb("wr_t", [P, KC, RS])
        a_col = sb("a_col", [P, 2, KC])
        a_diag = sb("a_diag", [P, KC, 2 * H])
        bias_row = sb("bias_row", [1, RS])
        we_row = sb("we_row", [P, H])
        stats = sb("stats", [P, T, 6])
        mom = sb("mom", [P, 3, T])
        rstd = sb("rstd", [P, T])
        nmr = sb("nmr", [P, T])
        hn = sb("hn", [P, 2, IN])
        h_t = sb("h_t", [P, 2, IN])
        h_row = sb("h_row", [P, 2, C])
        r_row = sb("r_row", [P, 2, IN])
        s_src = sb("s_src", [P, T, H])

        gath = sb("gath", [P, SLOTS * C])
        adj_t = sb("adj_t", [P, 2, N])
        seg_i = sb("seg_i", [P, NSEG, 8], I32)
        seg_base = sb("seg_base", [P, NSEG * 8])
        row_i = sb("row_i", [P, 1], I32)
        row_id = sb("row_id", [P, 1])
        top_v = sb("top_v", [P, NSEG * 8])
        top_j = sb("top_j", [P, NSEG * 8], U32)
        col = sb("col", [P, NSEG * 8])
        vpos = sb("vpos", [P, NSEG * 8])
        code = sb("code", [P, NSEG * 8], U32)
        key_hi = sb("key_hi", [P, NSEG * 8], U32)
        key_lo = sb("key_lo", [P, NSEG * 8], U32)
        list_hi = sb("list_hi", [P, SLOTS], U32)
        list_lo = sb("list_lo", [P, SLOTS], U32)
        nb = sb("nb", [P, SLOTS], U32)
        own = sb("own", [P, SLOTS])
        pen = sb("pen", [P, SLOTS])
        vhi = sb("vhi", [P, SLOTS], U32)
        vlist = sb("vlist", [P, SLOTS], U32)
        idx = sb("idx", [P, 2, SLOTS], U32)
        score0 = sb("score0", [P, 2, SLOTS * H])
        sgn = sb("sgn", [P, 2, CNT], BF16)
        npos = sb("npos", [P, 2, NCNT])
        kept = sb("kept", [P, 2])
        junk = sb("junk", [P, NSEG * 8])
        worst = sb("worst", [1, 2])
        cut = sb("cut", [1, 4])
        cum = sb("cum", [1, 4])
        plan = sb("plan", [1, 2, 4], U32)
        flags = sb("flags", [1, T])
        ords = sb("ords", [1, T + 1])
        todo = sb("todo", [1, T, 2], U32)
        z = sb("z", [P, 2, GS * H + H])
        corr = sb("corr", [P, 4, H])
        gmax = sb("gmax", [P, H])
        m = sb("m", [P, 2, H])
        acc = sb("acc", [P, C])
        rden = sb("rden", [P, H])
        r_in = sb("r_in", [P, 2, IN])
        o_buf = sb("o_buf", [P, 2, IN])
        v_in = sb("v_in", [P, CHUNK])

        p_tr = [ps(f"p_tr{i}", [P, IN]) for i in range(2)]
        p_a = [ps(f"p_a{i}", [P, C]) for i in range(2)]
        p_b = [ps(f"p_b{i}", [P, RS]) for i in range(2)]
        p_st = ps("p_st", [P, 2 * P])

        x_sb = gath[:, 0:T * IN].rearrange("p (t c) -> p t c", c=IN)
        slots = gath[:, :].rearrange("p (s c) -> p s c", c=C)
        cells = gath[:, :].rearrange("p (a e) -> p a e", e=E)

        w_in = sem("w_in")
        x_in = [sem(f"x_in{q}") for q in range(XQ)]
        consts = sem("consts")
        diag_ok = sem("diag_ok")
        wtr_ok = sem("wtr_ok")
        wtr_used = sem("wtr_used")
        var_ok = sem("var_ok")
        std_ok = sem("std_ok")
        norm_ok = sem("norm_ok")
        hn_ok = sem("hn_ok")
        tr_ok = sem("tr_ok")
        ht_ok = sem("ht_ok")
        mm_ok = sem("mm_ok")
        hrow_ok = sem("hrow_ok")
        rrow_ok = sem("rrow_ok")
        h_st = [sem(f"h_st{i}") for i in range(2)]
        r_st = [sem(f"r_st{i}") for i in range(2)]
        base_ok = sem("base_ok")
        adj_in = [sem(f"adj_in{i}") for i in range(2)]
        segs_done = sem("segs_done")
        count_ok = sem("count_ok")
        kept_ok = sem("kept_ok")
        worst_tr = sem("worst_tr")
        plan_self = sem("plan_self")
        list_ok = sem("list_ok")
        rows_in = [sem(f"rows_in{g}") for g in range(NG)]
        z_ok = sem("z_ok")
        p_ok = sem("p_ok")
        w_ok = sem("w_ok")
        sum_ok = sem("sum_ok")
        merged = sem("merged")
        r_ld = [sem(f"r_ld{i}") for i in range(2)]
        o_ok = sem("o_ok")
        o_st = [sem(f"o_st{i}") for i in range(2)]
        todo_ok = sem("todo_ok")
        sl_h = sem("sl_h")
        sl_v = sem("sl_v")
        sl_r = sem("sl_r")
        sl_z = sem("sl_z")
        sl_p = sem("sl_p")
        sl_w = sem("sl_w")
        sl_sum = sem("sl_sum")
        sl_free = sem("sl_free")
        sl_o = sem("sl_o")
        sl_st = sem("sl_st")
        passed = {k: sem(f"passed_{k}") for k in ("sp", "pool", "act", "dve", "pe")}

        def wait_reg(eng, name, sm, value):
            eng.wait_ge(sm, value)
            eng.sem_inc(passed[name], 1)

        block = ctx.enter_context(nc.Block())

        @block.sync
        def _(sp):
            for n, (dst, src) in enumerate(((w_nat, W), (wr_nat, Wr))):
                sp.dma_start(dst[:, :, :], src.rearrange("(c p) i -> p c i", p=P)).then_inc(w_in, 16)
            with nc.allow_non_contiguous_dma(reason="small vectors"):
                for n, a in enumerate((a_src, a_dst)):
                    for c in range(KC):
                        sp.dma_start(a_col[:, n, c:c + 1],
                                     a[c * HC:(c + 1) * HC, :].rearrange("h (d o) -> (h d) o", o=1)).then_inc(w_in, 16)
                sp.dma_start(we_row[:, :], We.rearrange("h o -> o h").partition_broadcast(P)).then_inc(w_in, 16)
            sp.dma_start(bias_row[0:1, IN:RS], be.rearrange("(o h) -> o h", o=1)).then_inc(w_in, 16)
            sp.dma_start(bias_row[0:1, 0:IN], br.rearrange("(o h) -> o h", o=1)).then_inc(w_in, 16)
            xt = x.rearrange("(t p) c -> p t c", p=P)
            for q in range(XQ):
                a, b = q * T // XQ, (q + 1) * T // XQ
                sp.dma_start(x_sb[:, a:b, :], xt[:, a:b, :]).then_inc(x_in[q], 16)
            for t in range(2):
                sp.dma_start(adj_t[:, t, :], adj[t * P:(t + 1) * P, :]).then_inc(adj_in[t], 16)
            with sp.Fori(0, T // 2) as i:
                for b in range(2):
                    wait_reg(sp, "sp", hrow_ok, 2 * i + b + 3)
                    sp.dma_start(h_rows[bass.ds((2 * i + b) * P, P), :], h_row[:, b, :]).then_inc(h_st[b], 16)
                    wait_reg(sp, "sp", rrow_ok, 2 * i + b + 3)
                    sp.dma_start(r_rows[bass.ds((2 * i + b) * P, P), :], r_row[:, b, :]).then_inc(r_st[b], 16)
            for b in range(2):
                sp.wait_ge(r_st[b], 16 * (T // 2) + 16)

            def load_r(t, b, n):
                wait_reg(sp, "sp", o_ok, t + 1)
                sp.dma_start(r_in[:, b, :], r_rows[bass.ds(t * P, P), :]).then_inc(r_ld[b], 16)

            def load_adj(t, b):
                wait_reg(sp, "sp", segs_done, t + 1)
                wait_reg(sp, "sp", count_ok, t + 1)
                sp.dma_start(adj_t[:, b, :], adj[bass.ds((t + 2) * P, P), :]).then_inc(adj_in[b], 16)

            def store_o(t, b):
                wait_reg(sp, "sp", o_ok, t + 3)
                sp.dma_start(out[bass.ds(t * P, P), :], o_buf[:, b, :]).then_inc(o_st[b], 16)

            load_r(0, 0, 0)
            load_adj(0, 0)
            with sp.Fori(0, T // 2 - 2) as i:
                for b in range(2):
                    t = 2 * i + 1 + b
                    load_r(t, 1 - b, 0)
                    load_adj(t, 1 - b)
                    store_o(t - 1, b)
            for t in range(T - 3, T):
                load_r(t, t % 2, 0)
                if t + 2 < T:
                    load_adj(t, t % 2)
                store_o(t - 1, (t - 1) % 2)
            store_o(T - 1, (T - 1) % 2)
            for b in range(2):
                sp.wait_ge(o_st[b], 16 * (T // 2) + 16)

            sp.wait_ge(todo_ok, 1)
            with sp.Fori(0, T) as t:
                flag = sp.value_load(todo[0:1, t, 0:1], min_val=0, max_val=1)
                nth = sp.value_load(todo[0:1, t, 1:2], min_val=0, max_val=T)
                with sp.If(flag > 0):
                    wait_reg(sp, "sp", sl_free, nth * NCH + 1)
                    sp.dma_start(r_in[:, 0, :], r_rows[bass.ds(t * P, P), :]).then_inc(sl_r, 16)
                    with sp.Fori(0, NCH) as i:
                        wait_reg(sp, "sp", sl_free, nth * NCH + i + 1)
                        sp.dma_start(slots[:, 0:CHUNK, :],
                                     h_rows[bass.ds(i * CHUNK, CHUNK), :].partition_broadcast(P)).then_inc(sl_h, 16)
                        sp.dma_start(v_in[:, :], adj[bass.ds(t * P, P), bass.ds(i * CHUNK, CHUNK)]).then_inc(sl_v, 16)
                    wait_reg(sp, "sp", sl_o, nth + 1)
                    sp.dma_start(out[bass.ds(t * P, P), :], o_buf[:, 0, :]).then_inc(sl_st, 16)
                    wait_reg(sp, "sp", sl_st, 16 * nth + 32)

        @block.gpsimd
        def _(pool):
            nc.gpsimd.memset(ident[:, :], 0.0).then_inc(base_ok, 1)
            nc.gpsimd.memset(gath[:, T * IN:SLOTS * C], 0.0).then_inc(consts, 1)
            nc.gpsimd.memset(ones[:, :], 1.0).then_inc(consts, 1)
            pool.wait_ge(base_ok, 1)
            nc.gpsimd.affine_select(out=ident[:, :], in_=ident[:, :], compare_op=ALU.not_equal, fill=1.0,
                                    base=0, pattern=[[-1, P]], channel_multiplier=1).then_inc(consts, 1)
            nc.gpsimd.iota(seg_i[:, :, :], [[SEG, NSEG], [0, 8]], base=CODE, channel_multiplier=0).then_inc(base_ok, 1)
            nc.gpsimd.iota(row_i[:, :], [[0, 1]], base=0, channel_multiplier=1).then_inc(base_ok, 1)
            for b in range(2):
                pool.wait_ge(h_st[b], 16 * (T // 2) + 16)
                pool.wait_ge(r_st[b], 16 * (T // 2) + 16)

            def gather(b, s):
                pool.indirect_dma_start(slots[:, s, :], None, h_rows[:, :],
                                        bass.IndirectOffsetOnAxis(ap=idx[:, b, s:s + 1], axis=0)
                                        ).then_inc(rows_in[s // GS], 16)

            def gather_tile(t, b):
                wait_reg(pool, "pool", list_ok, t + 1)
                longest = pool.value_load(plan[0:1, b, 0:1], min_val=0, max_val=SLOTS)
                for s in range(SLOTS):
                    if s < FIRM * GS:
                        if s % GS == 0:
                            wait_reg(pool, "pool", sum_ok, NG * t + s // GS + 1)
                        gather(b, s)
                    else:
                        with pool.If(longest > s):
                            if s % GS == 0:
                                wait_reg(pool, "pool", sum_ok, NG * t + s // GS + 1)
                            gather(b, s)

            with pool.Fori(0, T // 2) as i:
                for b in range(2):
                    gather_tile(2 * i + b, b)

        @block.scalar
        def _(act):
            act.wait_ge(var_ok, 1)
            nc.scalar.activation(rstd[:, :], mom[:, 1, :], ACT.Sqrt).then_inc(std_ok, 1)
            act.wait_ge(norm_ok, 1)

            def norm(t, b):
                wait_reg(act, "act", tr_ok, t + 1)
                nc.scalar.activation(hn[:, b, :], x_sb[:, t, :], ACT.Relu, scale=rstd[:, bass.ds(t, 1)],
                                     bias=nmr[:, bass.ds(t, 1)]).then_inc(hn_ok, 1)

            norm(0, 0)

            def evacuate(t, b, i):
                wait_reg(act, "act", mm_ok, t + 3)
                wait_reg(act, "act", h_st[b], 16 * i + 16)
                nc.scalar.activation(h_row[:, b, :], p_a[b][:, 0:C], ACT.Copy).then_inc(hrow_ok, 1)

            with act.Fori(0, T // 2 - 1) as i:
                for b in range(2):
                    norm(2 * i + b + 1, 1 - b)
                    evacuate(2 * i + b, b, i)
            norm(T - 1, 1)
            evacuate(T - 2, 0, T // 2 - 1)
            evacuate(T - 1, 1, T // 2 - 1)

            def count(t, b, loads):
                wait_reg(act, "act", adj_in[b], loads)
                wait_reg(act, "act", kept_ok, t + 1)
                for q in range(NCNT):
                    if q >= 2:
                        act.drain()
                    nc.scalar.activation(sgn[:, q % 2, :], adj_t[:, b, q * CNT:(q + 1) * CNT], ACT.Relu)
                    act.drain()
                    last = nc.scalar.activation(sgn[:, q % 2, :], sgn[:, q % 2, :], ACT.Sign,
                                                accum_out=npos[:, b, q:q + 1])
                last.then_inc(count_ok, 1)

            def exps(t):
                for g in range(NG):
                    wait_reg(act, "act", z_ok, NG * t + g + 1)
                    nc.scalar.activation(cells[:, g * GS * H:(g + 1) * GS * H, D], z[:, g % 2, 0:GS * H], ACT.Exp)
                    nc.scalar.activation(corr[:, g % 4, :], z[:, g % 2, GS * H:], ACT.Exp).then_inc(p_ok, 1)

            count(0, 0, 16)
            with act.Fori(0, T // 2 - 1) as i:
                count(2 * i + 1, 1, 16 * i + 16)
                exps(2 * i)
                count(2 * i + 2, 0, 16 * i + 32)
                exps(2 * i + 1)
            count(T - 1, 1, 16 * (T // 2))
            exps(T - 2)
            exps(T - 1)

            act.wait_ge(todo_ok, 1)
            with act.Fori(0, T) as t:
                flag = act.value_load(todo[0:1, t, 0:1], min_val=0, max_val=1)
                nth = act.value_load(todo[0:1, t, 1:2], min_val=0, max_val=T)
                with act.If(flag > 0):
                    with act.Fori(0, NCH) as i:
                        wait_reg(act, "act", sl_z, nth * NCH + i + 1)
                        nc.scalar.activation(cells[:, 0:CHUNK * H, D], score0[:, 0, :], ACT.Exp)
                        nc.scalar.activation(corr[:, 0, :], z[:, 0, GS * H:], ACT.Exp).then_inc(sl_p, 1)

        @block.tensor
        def _(pe):
            pe.wait_ge(consts, 3)
            pe.wait_ge(w_in, 16 * (5 + 2 * KC))
            n = 0
            for nat in (w_nat, wr_nat):
                for c in range(KC):
                    for k in range(KC):
                        if n >= 2:
                            pe.wait_ge(wtr_used, n - 1)
                        nc.tensor.transpose(p_tr[n % 2][:, 0:P], nat[:, c, k * P:(k + 1) * P],
                                            ident[:, :]).then_inc(wtr_ok, 1)
                        n += 1
            pe.wait_ge(diag_ok, 1)
            for k in range(KC):
                for c in range(KC):
                    last = nc.tensor.matmul(p_b[k][:, 0:2 * H], w_nat[:, c, k * P:(k + 1) * P], a_diag[:, c, :],
                                            start=(c == 0), stop=(c == KC - 1))
                last.then_inc(wtr_ok, 1)
            pe.wait_ge(wtr_used, n + KC)

            def tr(t, b):
                wait_reg(pe, "pe", hn_ok, t + 1)
                wait_reg(pe, "pe", ht_ok, t + 1)
                for k in range(KC):
                    last = nc.tensor.transpose(p_tr[b][:, k * P:(k + 1) * P], hn[:, b, k * P:(k + 1) * P], ident[:, :])
                last.then_inc(tr_ok, 1)

            tr(0, 0)

            def project(t, b):
                wait_reg(pe, "pe", ht_ok, t + 3)
                wait_reg(pe, "pe", hrow_ok, t + 1)
                wait_reg(pe, "pe", rrow_ok, t + 1)
                for k in range(KC):
                    nc.tensor.matmul(p_a[b][:, :], h_t[:, b, k * P:(k + 1) * P], w_t[:, k, :],
                                     start=(k == 0), stop=(k == KC - 1))
                for k in range(KC):
                    nc.tensor.matmul(p_b[b][:, :], h_t[:, b, k * P:(k + 1) * P], wr_t[:, k, :],
                                     start=(k == 0), stop=False)
                last = nc.tensor.matmul(p_b[b][:, :], ones[0:1, :], bias_row[0:1, :], start=False, stop=True)
                last.then_inc(mm_ok, 1)

            with pe.Fori(0, T // 2 - 1) as i:
                for b in range(2):
                    tr(2 * i + b + 1, 1 - b)
                    project(2 * i + b, b)
            tr(T - 1, 1)
            project(T - 2, 0)
            project(T - 1, 1)

            def turn(t):
                wait_reg(pe, "pe", kept_ok, t + 3)
                nc.tensor.transpose(p_st[0:1, 0:P], kept[:, 0:1], ident[:, :])
                nc.tensor.transpose(p_st[0:1, P:2 * P], kept[:, 1:2], ident[:, :]).then_inc(worst_tr, 1)

            def sums(t):
                for g in range(NG):
                    wait_reg(pe, "pe", merged, NG * t + g + 1)
                    wait_reg(pe, "pe", p_ok, NG * t + g + 2)
                    wait_reg(pe, "pe", w_ok, NG * t + g + 1)
                    for s in range(GS):
                        last = nc.tensor.matmul(p_a[g % 2][:, 0:C], ident[:, :], slots[:, g * GS + s, :],
                                                start=(s == 0), stop=(s == GS - 1))
                    last.then_inc(sum_ok, 1)

            turn(0)
            with pe.Fori(0, T - 1) as t:
                turn(t + 1)
                sums(t)
            sums(T - 1)

            pe.wait_ge(todo_ok, 1)
            with pe.Fori(0, T) as t:
                flag = pe.value_load(todo[0:1, t, 0:1], min_val=0, max_val=1)
                nth = pe.value_load(todo[0:1, t, 1:2], min_val=0, max_val=T)
                with pe.If(flag > 0):
                    with pe.Fori(0, NCH) as i:
                        wait_reg(pe, "pe", sl_p, nth * NCH + i + 1)
                        wait_reg(pe, "pe", sl_w, nth * NCH + i + 1)
                        for s in range(CHUNK):
                            last = nc.tensor.matmul(p_a[0][:, 0:C], ident[:, :], slots[:, s, :],
                                                    start=(s == 0), stop=(s == CHUNK - 1))
                        last.then_inc(sl_sum, 1)

        @block.vector
        def _(v):
            V = nc.vector

            def bc(ap, shape, axis):
                return ap.unsqueeze(axis).broadcast_to(shape)

            for sm, n in ((tr_ok, 2), (ht_ok, 2), (mm_ok, 2), (hrow_ok, 2), (rrow_ok, 2), (kept_ok, 2),
                          (merged, 2), (o_ok, 2), (sum_ok, NG), (p_ok, 1), (sl_free, 1), (sl_st, 16),
                          *((st, 16) for st in (*h_st, *r_st, *o_st))):
                v.sem_inc(sm, n)
            V.memset(a_diag[:, :, :], 0.0)
            V.memset(cum[:, :], 0.0)
            V.memset(z[:, :, :], 0.0)
            V.memset(ords[:, :], 0.0)
            v.wait_ge(w_in, 16 * (5 + 2 * KC))
            v.drain()
            for n in range(2):
                for c in range(KC):
                    for q in range(HC):
                        r = slice(q * D, (q + 1) * D)
                        last = V.tensor_copy(a_diag[r, c, n * H + c * HC + q:n * H + c * HC + q + 1],
                                             a_col[r, n, c:c + 1])
            last.then_inc(diag_ok, 1)
            heads = w_t[:, :, 0:C].rearrange("p k (h e) -> p k h e", e=E)
            n = 0
            for is_r in range(2):
                for c in range(KC):
                    for k in range(KC):
                        v.wait_ge(wtr_ok, n + 1)
                        if is_r:
                            V.tensor_copy(wr_t[:, k, c * P:(c + 1) * P], p_tr[n % 2][:, 0:P]).then_inc(wtr_used, 1)
                        else:
                            V.tensor_copy(heads[:, k, c * HC:(c + 1) * HC, 0:D],
                                          p_tr[n % 2][:, 0:P].rearrange("p (h d) -> p h d", d=D)).then_inc(wtr_used, 1)
                        n += 1
            for k in range(KC):
                v.wait_ge(wtr_ok, n + k + 1)
                V.tensor_copy(wr_t[:, k, IN:RS], p_b[k][:, 0:H])
                V.tensor_copy(heads[:, k, :, D], p_b[k][:, H:2 * H]).then_inc(wtr_used, 1)

            for q in range(XQ):
                v.wait_ge(x_in[q], 16)
                with v.Fori(q * T // XQ, (q + 1) * T // XQ) as t:
                    V.bn_stats(stats[:, t, :], x_sb[:, t, :])
            v.drain()
            V.tensor_tensor(mom[:, 0, :], stats[:, :, 1], stats[:, :, 4], ALU.add)
            V.tensor_tensor(mom[:, 1, :], stats[:, :, 2], stats[:, :, 5], ALU.add)
            V.tensor_tensor(mom[:, 2, :], stats[:, :, 1], stats[:, :, 4], ALU.subtract)
            v.drain()
            V.tensor_tensor(mom[:, 2, :], mom[:, 2, :], mom[:, 2, :], ALU.mult)
            V.tensor_scalar(mom[:, 0, :], mom[:, 0, :], 0.5, None, ALU.mult)
            V.tensor_scalar(mom[:, 1, :], mom[:, 1, :], 1.0 / IN, EPS, ALU.mult, ALU.add)
            v.drain()
            V.scalar_tensor_tensor(mom[:, 1, :], mom[:, 2, :], 0.25, mom[:, 1, :], ALU.mult, ALU.add).then_inc(var_ok, 1)
            v.wait_ge(std_ok, 1)
            V.reciprocal(rstd[:, :], rstd[:, :])
            v.drain()
            V.scalar_tensor_tensor(nmr[:, :], mom[:, 0, :], -1.0, rstd[:, :], ALU.mult, ALU.mult).then_inc(norm_ok, 1)

            with v.Fori(0, T // 2) as i:
                for b in range(2):
                    t = 2 * i + b
                    wait_reg(v, "dve", tr_ok, t + 3)
                    wait_reg(v, "dve", mm_ok, t + 1)
                    V.tensor_copy(h_t[:, b, :], p_tr[b][:, :]).then_inc(ht_ok, 1)
                    wait_reg(v, "dve", mm_ok, t + 3)
                    wait_reg(v, "dve", r_st[b], 16 * i + 16)
                    V.tensor_copy(s_src[:, t, :], p_b[b][:, IN:RS])
                    V.tensor_tensor(r_row[:, b, :], p_b[b][:, 0:IN], x_sb[:, t, :], ALU.add).then_inc(rrow_ok, 1)

            v.wait_ge(base_ok, 3)
            V.tensor_copy(seg_base[:, :], seg_i[:, :, :].rearrange("p n k -> p (n k)"))
            V.tensor_copy(row_id[:, :], row_i[:, :])

            def f(ap):
                return ap.bitcast(F32)

            def pack(t, b, loads):
                wait_reg(v, "dve", adj_in[b], loads)
                for n in range(NSEG):
                    V.max(top_v[:, 8 * n:8 * n + 8], adj_t[:, b, n * SEG:(n + 1) * SEG])
                v.drain()
                for n in range(NSEG):
                    last = V.max_index(top_j[:, 8 * n:8 * n + 8], top_v[:, 8 * n:8 * n + 8],
                                       adj_t[:, b, n * SEG:(n + 1) * SEG])
                last.then_inc(segs_done, 1)
                v.drain()
                V.tensor_tensor(col[:, :], top_j[:, :], seg_base[:, :], ALU.add)
                V.tensor_scalar(vpos[:, :], top_v[:, :], 0.0, None, ALU.max)
                V.tensor_scalar(junk[:, :], top_v[:, :], 0.0, 0.0, ALU.is_gt, ALU.add, accum_out=kept[:, 0:1])
                v.drain()
                V.scalar_tensor_tensor(code[:, :], vpos[:, :], 0.0, col[:, :], ALU.is_gt, ALU.mult)
                wait_reg(v, "dve", count_ok, t + 1)
                V.tensor_reduce(kept[:, 1:2], npos[:, b, :], axis=AX.X, op=ALU.add)
                v.drain()
                V.tensor_scalar(key_hi[:, :], code[:, :], 16, None, ALU.logical_shift_left)
                V.tensor_tensor(kept[:, 1:2], kept[:, 1:2], kept[:, 0:1], ALU.not_equal)
                v.drain()
                V.scalar_tensor_tensor(kept[:, 1:2], kept[:, 0:1], float(SLOTS), kept[:, 1:2],
                                       ALU.is_gt, ALU.max).then_inc(kept_ok, 1)
                bits = vpos[:, :].bitcast(U32)
                V.scalar_tensor_tensor(key_lo[:, :], bits, 0xFFFF, key_hi[:, :], ALU.bitwise_and, ALU.bitwise_or)
                v.drain()
                V.scalar_tensor_tensor(key_hi[:, :], bits, 16, key_hi[:, :], ALU.logical_shift_right, ALU.bitwise_or)
                v.drain()
                for r in range(NG):
                    s = slice(8 * r, 8 * r + 8)
                    for lst, key in ((list_hi, key_hi), (list_lo, key_lo)):
                        V.max(f(lst[:, s]), f(key[:, :]))
                    if r < NG - 1:
                        v.drain()
                        for lst, key in ((list_hi, key_hi), (list_lo, key_lo)):
                            V.match_replace(f(key[:, :]), f(lst[:, s]), f(key[:, :]), 0.0)
                    v.drain()
                V.tensor_scalar(nb[:, :], list_hi[:, :], 16, CODE - 1, ALU.logical_shift_right, ALU.bitwise_and)
                V.tensor_scalar(vhi[:, :], list_hi[:, :], 0xFFFF, 16, ALU.bitwise_and, ALU.logical_shift_left)
                V.tensor_scalar(own[:, :], f(list_hi[:, :]), 0.0, row_id[:, 0:1], ALU.is_equal, ALU.mult)
                V.tensor_scalar(pen[:, :], f(list_hi[:, :]), 0.0, PAD, ALU.is_equal, ALU.mult)
                v.drain()
                V.scalar_tensor_tensor(vlist[:, :], list_lo[:, :], 0xFFFF, vhi[:, :], ALU.bitwise_and, ALU.bitwise_or)
                V.tensor_tensor(idx[:, b, :], nb[:, :], own[:, :], ALU.add)
                V.tensor_scalar(row_id[:, :], row_id[:, :], float(P), None, ALU.add)
                v.drain()
                s3 = [P, SLOTS, H]
                s0 = score0[:, b, :].rearrange("p (s h) -> p s h", h=H)
                V.tensor_tensor(s0, bc(f(vlist[:, :]), s3, 2), bc(we_row[:, :], s3, 1), ALU.mult)
                v.drain()
                V.tensor_tensor(s0, s0, s_src[:, bass.ds(t, 1), :].broadcast_to(s3), ALU.add)
                v.drain()
                V.tensor_tensor(s0, s0, bc(pen[:, :], s3, 2), ALU.add)
                wait_reg(v, "dve", worst_tr, t + 1)
                V.tensor_reduce(worst[:, :], p_st[0:1, :].rearrange("p (a q) -> p a q", q=P), axis=AX.X, op=ALU.max)
                v.drain()
                V.tensor_copy(flags[0:1, bass.ds(t, 1)], worst[:, 1:2])
                V.tensor_scalar(cut[:, 0:1], worst[:, 0:1], float(SLOTS), None, ALU.min)
                v.drain()
                for n, g in enumerate(range(FIRM, NG)):
                    V.tensor_scalar(cut[:, n + 1:n + 2], cut[:, 0:1], float(-GS * g), 0.0, ALU.add, ALU.max)
                v.drain()
                V.tensor_scalar(cut[:, 1:], cut[:, 1:], float(GS), 16.0, ALU.min, ALU.mult)
                v.drain()
                V.tensor_tensor(cum[:, 1:], cum[:, 1:], cut[:, 1:], ALU.add)
                V.tensor_copy(cum[:, 0:1], cut[:, 0:1])
                v.drain()
                V.tensor_copy(plan[:, b, :], cum[:, :]).then_inc(list_ok, 1)

            def score(t, b, g, arrived):
                wait_reg(v, "dve", rows_in[g], arrived)
                zz = z[:, g % 2, 0:GS * H]
                V.tensor_tensor(zz, score0[:, b, g * GS * H:(g + 1) * GS * H],
                                cells[:, g * GS * H:(g + 1) * GS * H, D], ALU.add)
                v.drain()
                V.scalar_tensor_tensor(zz, zz, ALPHA, zz, ALU.mult, ALU.max)
                v.drain()
                V.tensor_reduce(gmax[:, :], zz.rearrange("p (s h) -> p h s", h=H), axis=AX.X, op=ALU.max)
                v.drain()
                if g == 0:
                    V.tensor_scalar(m[:, 0, :], gmax[:, :], FLOOR, None, ALU.max)
                else:
                    V.tensor_tensor(m[:, g % 2, :], gmax[:, :], m[:, (g - 1) % 2, :], ALU.max)
                v.drain()
                if g:
                    V.tensor_tensor(z[:, g % 2, GS * H:], m[:, (g - 1) % 2, :], m[:, g % 2, :], ALU.subtract)
                z3 = zz.rearrange("p (s h) -> p s h", h=H)
                V.tensor_tensor(z3, z3, bc(m[:, g % 2, :], [P, GS, H], 1), ALU.subtract).then_inc(z_ok, 1)

            def weigh(t, g):
                wait_reg(v, "dve", p_ok, NG * t + g + 2)
                a = slice(g * GS * H, (g + 1) * GS * H)
                V.tensor_tensor(cells[:, a, 0:D], cells[:, a, 0:D],
                                cells[:, a, D:E].broadcast_to([P, GS * H, D]), ALU.mult).then_inc(w_ok, 1)

            def merge(t, g):
                wait_reg(v, "dve", sum_ok, NG * t + g + 1 + NG)
                if g == 0:
                    V.tensor_copy(acc[:, :], p_a[0][:, 0:C]).then_inc(merged, 1)
                    return
                v.drain()
                a3 = acc[:, :].rearrange("p (h e) -> p h e", e=E)
                V.tensor_tensor(a3, a3, bc(corr[:, g % 4, :], [P, H, E], 2), ALU.mult)
                v.drain()
                V.tensor_tensor(acc[:, :], acc[:, :], p_a[g % 2][:, 0:C], ALU.add).then_inc(merged, 1)

            def attend(t, b, i):
                plan_regs = [v.value_load(plan[0:1, b, n:n + 1], min_val=0, max_val=SLOTS if n == 0 else 16 * GS * T)
                             for n in range(1 + NG - FIRM)]
                longest = plan_regs[0]
                wait_reg(v, "dve", p_ok, NG * t + 1)
                for g in range(NG + 2):
                    if g < FIRM:
                        score(t, b, g, (t + 1) * 16 * GS)
                    elif g < NG:
                        with v.If(longest > g * GS):
                            score(t, b, g, plan_regs[1 + g - FIRM])
                        with v.Else():
                            v.drain().then_inc(z_ok, 1)
                    q = g - 1
                    if 0 <= q < FIRM:
                        weigh(t, q)
                    elif FIRM <= q < NG:
                        with v.If(longest > q * GS):
                            weigh(t, q)
                        with v.Else():
                            v.drain().then_inc(w_ok, 1)
                    q = g - 2
                    if 0 <= q < FIRM:
                        merge(t, q)
                    elif FIRM <= q < NG:
                        with v.If(longest > q * GS):
                            merge(t, q)
                        with v.Else():
                            v.drain().then_inc(merged, 1)
                v.drain()
                wait_reg(v, "dve", r_ld[b], 16 * i + 16)
                wait_reg(v, "dve", o_st[b], 16 * i + 16)
                finish(b, o_ok)

            def finish(b, done):
                a3 = acc[:, :].rearrange("p (h e) -> p h e", e=E)
                V.reciprocal(rden[:, :], a3[:, :, D])
                v.drain()
                V.tensor_tensor(o_buf[:, b, :].rearrange("p (h d) -> p h d", d=D), a3[:, :, 0:D],
                                bc(rden[:, :], [P, H, D], 2), ALU.mult)
                v.drain()
                V.tensor_tensor(o_buf[:, b, :], o_buf[:, b, :], r_in[:, b, :], ALU.add).then_inc(done, 1)

            v.drain()
            pack(0, 0, 16)
            with v.Fori(0, T // 2 - 1) as i:
                pack(2 * i + 1, 1, 16 * i + 16)
                attend(2 * i, 0, i)
                pack(2 * i + 2, 0, 16 * i + 32)
                attend(2 * i + 1, 1, i)
            pack(T - 1, 1, 16 * (T // 2))
            attend(T - 2, 0, T // 2 - 1)
            attend(T - 1, 1, T // 2 - 1)

            v.drain()
            V.tensor_tensor_scan(ords[0:1, 1:], flags[0:1, :], flags[0:1, :], 0.0, ALU.add, ALU.bypass)
            V.tensor_copy(todo[0:1, :, 0], flags[0:1, :])
            v.drain()
            V.tensor_copy(todo[0:1, :, 1], ords[0:1, 0:T]).then_inc(todo_ok, 1)
            v.wait_ge(p_ok, NG * T + 1)
            v.wait_ge(sum_ok, NG * T + NG)
            v.wait_ge(todo_ok, 1)
            with v.Fori(0, T) as t:
                flag = v.value_load(todo[0:1, t, 0:1], min_val=0, max_val=1)
                nth = v.value_load(todo[0:1, t, 1:2], min_val=0, max_val=T)
                with v.If(flag > 0):
                    V.memset(m[:, 0, :], FLOOR)
                    V.memset(acc[:, :], 0.0)
                    with v.Fori(0, NCH) as i:
                        n = nth * NCH + i
                        s3 = [P, CHUNK, H]
                        s0 = score0[:, 0, :].rearrange("p (s h) -> p s h", h=H)
                        a3 = acc[:, :].rearrange("p (h e) -> p h e", e=E)
                        wait_reg(v, "dve", sl_v, 16 * n + 16)
                        V.tensor_tensor(s0, bc(v_in[:, :], s3, 2), bc(we_row[:, :], s3, 1), ALU.mult)
                        V.tensor_scalar(pen[:, :], v_in[:, :], 0.0, PAD, ALU.is_le, ALU.mult)
                        v.drain()
                        V.tensor_tensor(s0, s0, s_src[:, bass.ds(t, 1), :].broadcast_to(s3), ALU.add)
                        wait_reg(v, "dve", sl_h, 16 * n + 16)
                        v.drain()
                        V.tensor_tensor(score0[:, 0, :], score0[:, 0, :], cells[:, 0:CHUNK * H, D], ALU.add)
                        v.drain()
                        V.tensor_tensor(s0, s0, bc(pen[:, :], s3, 2), ALU.add)
                        v.drain()
                        V.scalar_tensor_tensor(s0, s0, ALPHA, s0, ALU.mult, ALU.max)
                        v.drain()
                        V.tensor_reduce(gmax[:, :], s0.rearrange("p s h -> p h s"), axis=AX.X, op=ALU.max)
                        v.drain()
                        V.tensor_tensor(m[:, 1, :], gmax[:, :], m[:, 0, :], ALU.max)
                        v.drain()
                        V.tensor_tensor(z[:, 0, GS * H:], m[:, 0, :], m[:, 1, :], ALU.subtract)
                        v.drain()
                        V.tensor_copy(m[:, 0, :], m[:, 1, :])
                        V.tensor_tensor(s0, s0, bc(m[:, 1, :], s3, 1), ALU.subtract).then_inc(sl_z, 1)
                        wait_reg(v, "dve", sl_p, n + 1)
                        V.tensor_tensor(cells[:, :, 0:D], cells[:, :, 0:D],
                                        cells[:, :, D:E].broadcast_to([P, CHUNK * H, D]), ALU.mult).then_inc(sl_w, 1)
                        V.tensor_tensor(a3, a3, bc(corr[:, 0, :], [P, H, E], 2), ALU.mult)
                        wait_reg(v, "dve", sl_sum, n + 1)
                        v.drain()
                        V.tensor_tensor(acc[:, :], acc[:, :], p_a[0][:, 0:C], ALU.add).then_inc(sl_free, 1)
                    v.drain()
                    wait_reg(v, "dve", sl_r, 16 * nth + 16)
                    wait_reg(v, "dve", sl_st, 16 * nth + 16)
                    finish(0, sl_o)
                    v.drain()


_INS = ["x", "adj", "L0_gnn_W", "L0_gnn_We", "L0_gnn_be", "L0_gnn_a_src", "L0_gnn_a_dst", "L0_gnn_Wr", "L0_gnn_br"]


def kernel(**inputs):
    import numpy as _np
    import concourse.bacc as _bacc
    from concourse import mybir as _mybir
    from concourse.bass_utils import run_bass_kernel_spmd as _run

    nc = _bacc.Bacc("TRN2", target_bir_lowering=False, num_devices=1)
    arrays, args = {}, []
    for name in _INS:
        a = _np.ascontiguousarray(inputs[name])
        arrays[f"in_{name}_dram"] = a
        args.append(nc.dram_tensor(f"in_{name}_dram", a.shape, _mybir.dt.from_np(a.dtype), kind="ExternalInput").ap())
    args.append(nc.dram_tensor("out_0_dram", inputs["x"].shape, _mybir.dt.float32, kind="ExternalOutput").ap())
    build(nc, *args)
    r = _run(nc, [arrays], core_ids=[0])
    return r.results[0]["out_0_dram"]
```

```python
import concourse.bass as bass
from concourse import mybir
from contextlib import ExitStack

F32 = mybir.dt.float32
BF16 = mybir.dt.bfloat16
U32 = mybir.dt.uint32
I32 = mybir.dt.int32
ALU = mybir.AluOpType
ACT = mybir.ActivationFunctionType
AX = mybir.AxisListType

P = 128
ALPHA = 0.2
EPS = 1e-5
SEG = 256
SLOTS = 64
SHORT = 48
FIRM = 40
GS = 16
NG = SLOTS // GS
NS = SHORT // GS
ROWS = 2 * SHORT + SLOTS - SHORT
CODE = 8192
PAD = -3.0e38
FLOOR = -5.0e37
CHUNK = 64
MAIN, SLOW = 0, 1


def build(nc, x, adj, W, We, be, a_src, a_dst, Wr, br, out):
    N, IN = x.shape
    H, D = a_src.shape
    E = D + 1
    C = H * E
    RS = IN + H
    T = N // P
    NSEG = N // SEG
    KC = IN // P
    HC = H // KC
    XQ = 4
    CNT = 1024
    NCNT = N // CNT
    NCH = N // CHUNK

    h_rows = nc.dram_tensor("h_rows", (N, C), F32, kind="Internal").ap()
    r_rows = nc.dram_tensor("r_rows", (N, IN), F32, kind="Internal").ap()

    ctx = ExitStack()
    with ctx:
        def sb(name, shape, dt=F32):
            return ctx.enter_context(nc.sbuf_tensor(name, shape, dt))

        def ps(name, shape):
            return ctx.enter_context(nc.psum_tensor(name, shape, F32))

        def sem(name):
            return ctx.enter_context(nc.semaphore(name))

        ident = sb("ident", [P, P])
        a_col = sb("a_col", [P, 2, KC])
        a_diag = sb("a_diag", [P, KC, 2 * H])
        we_row = sb("we_row", [P, H])
        s_src = sb("s_src", [P, T, H])

        gath = sb("gath", [P, ROWS * C])

        used = [T * IN]

        def before(*shape):
            n = 1
            for k in shape:
                n *= k
            used[0] += n
            flat = gath[:, used[0] - n:used[0]]
            return flat.rearrange("p (a b) -> p a b", a=shape[0]) if len(shape) == 2 else flat

        w_nat, wr_nat = before(KC, IN), before(KC, IN)
        w_t, wr_t = before(KC, C), before(KC, RS)
        stats = before(T, 6)
        hn, h_t, r_row = before(2, IN), before(2, IN), before(2, IN)
        h_row = before(2, C)
        mom, rstd, nmr = before(3, T), before(T), before(T)
        seg_i = before(NSEG, 8).bitcast(I32)
        ones, bias_row = before(P)[0:1, :], before(RS)[0:1, :]
        adj_t = sb("adj_t", [P, 2, N])
        seg_base = sb("seg_base", [P, NSEG * 8])
        row_i = sb("row_i", [P, 1], I32)
        row_id = sb("row_id", [P, 1])
        top_v = sb("top_v", [P, NSEG * 8])
        top_j = sb("top_j", [P, NSEG * 8], U32)
        vpos = sb("vpos", [P, NSEG * 8])
        code = sb("code", [P, NSEG * 8], U32)
        key_hi = sb("key_hi", [P, NSEG * 8], U32)
        key_lo = sb("key_lo", [P, NSEG * 8], U32)
        col = key_lo[:, :].bitcast(F32)
        junk = key_hi[:, :].bitcast(F32)
        list_hi = sb("list_hi", [P, SLOTS], U32)
        list_lo = sb("list_lo", [P, SLOTS], U32)
        nb = sb("nb", [P, SLOTS], U32)
        own = sb("own", [P, SLOTS])
        pen = sb("pen", [P, 2, SLOTS])
        vhi = sb("vhi", [P, SLOTS], U32)
        vlist = sb("vlist", [P, 2, SLOTS], U32)
        idx = sb("idx", [P, 2, SLOTS], U32)
        score0 = sb("score0", [P, 2, SLOTS * H])
        sgn = sb("sgn", [P, CNT], BF16)
        npos = sb("npos", [P, 2, NCNT])
        kept = sb("kept", [P, 2])
        worst = sb("worst", [1, 2])
        cut = sb("cut", [1, 3])
        cum = sb("cum", [1, 2, 3])
        plan = sb("plan", [1, 2, 3], U32)
        flags = sb("flags", [1, T])
        ords = sb("ords", [1, T + 1])
        todo = sb("todo", [1, T, 2], U32)
        total = sb("total", [1, 1], U32)
        z = sb("z", [P, SLOTS * H])
        dmax = sb("dmax", [P, H])
        corr = sb("corr", [P, H])
        gmax = sb("gmax", [P, H])
        m = sb("m", [P, 2, H])
        acc = z[:, 0:C]
        rden = sb("rden", [P, H])
        r_in = sb("r_in", [P, 2, IN])
        o_buf = sb("o_buf", [P, 2, IN])
        v_in = sb("v_in", [P, CHUNK])

        p_tr = [ps(f"p_tr{i}", [P, IN]) for i in range(2)]
        p_a = [ps(f"p_a{i}", [P, C]) for i in range(2)]
        p_b = [ps(f"p_b{i}", [P, RS]) for i in range(2)]
        p_st = ps("p_st", [P, 2 * P])

        x_sb = gath[:, 0:T * IN].rearrange("p (t c) -> p t c", c=IN)
        slots = gath[:, :].rearrange("p (s c) -> p s c", c=C)
        cells = gath[:, :].rearrange("p (a e) -> p a e", e=E)

        def row(b, s):
            return b * SHORT + s if s < SHORT else SHORT + s

        w_in = sem("w_in")
        x_in = [sem(f"x_in{q}") for q in range(XQ)]
        consts = sem("consts")
        diag_ok = sem("diag_ok")
        wtr_ok = sem("wtr_ok")
        wtr_used = sem("wtr_used")
        var_ok = sem("var_ok")
        std_ok = sem("std_ok")
        norm_ok = sem("norm_ok")
        hn_ok = sem("hn_ok")
        tr_ok = sem("tr_ok")
        ht_ok = sem("ht_ok")
        mm_ok = sem("mm_ok")
        hrow_ok = sem("hrow_ok")
        rrow_ok = sem("rrow_ok")
        h_st = [sem(f"h_st{i}") for i in range(2)]
        r_st = [sem(f"r_st{i}") for i in range(2)]
        base_ok = sem("base_ok")
        adj_in = [sem(f"adj_in{i}") for i in range(2)]
        segs_done = sem("segs_done")
        count_ok = sem("count_ok")
        kept_ok = sem("kept_ok")
        worst_tr = sem("worst_tr")
        plan_self = sem("plan_self")
        list_ok = sem("list_ok")
        rows_in = [[sem(f"rows_in{b}_{g}") for g in range(NG)] for b in range(2)]
        z_ok = sem("z_ok")
        p_ok = sem("p_ok")
        w_ok = sem("w_ok")
        sum_ok = sem("sum_ok")
        done = sem("done")
        v_ok = sem("v_ok")
        score0_ok = sem("score0_ok")
        r_ld = [sem(f"r_ld{i}") for i in range(2)]
        o_ok = sem("o_ok")
        o_st = [sem(f"o_st{i}") for i in range(2)]
        todo_ok = sem("todo_ok")
        sl_h = sem("sl_h")
        sl_v = sem("sl_v")
        sl_r = sem("sl_r")
        sl_z = sem("sl_z")
        sl_p = sem("sl_p")
        sl_w = sem("sl_w")
        sl_sum = sem("sl_sum")
        sl_free = sem("sl_free")
        sl_o = sem("sl_o")
        sl_st = sem("sl_st")
        passed = {k: sem(f"passed_{k}") for k in ("sp", "pool", "act", "dve", "pe")}

        def wait_reg(eng, name, sm, value):
            eng.wait_ge(sm, value)
            eng.sem_inc(passed[name], 1)

        block = ctx.enter_context(nc.Block())

        @block.sync
        def _(sp):
            for n, (dst, src) in enumerate(((w_nat, W), (wr_nat, Wr))):
                sp.dma_start(dst[:, :, :], src.rearrange("(c p) i -> p c i", p=P)).then_inc(w_in, 16)
            with nc.allow_non_contiguous_dma(reason="small vectors"):
                for n, a in enumerate((a_src, a_dst)):
                    for c in range(KC):
                        sp.dma_start(a_col[:, n, c:c + 1],
                                     a[c * HC:(c + 1) * HC, :].rearrange("h (d o) -> (h d) o", o=1)).then_inc(w_in, 16)
                sp.dma_start(we_row[:, :], We.rearrange("h o -> o h").partition_broadcast(P)).then_inc(w_in, 16)
            sp.dma_start(bias_row[0:1, IN:RS], be.rearrange("(o h) -> o h", o=1)).then_inc(w_in, 16)
            sp.dma_start(bias_row[0:1, 0:IN], br.rearrange("(o h) -> o h", o=1)).then_inc(w_in, 16)
            xt = x.rearrange("(t p) c -> p t c", p=P)
            for q in range(XQ):
                a, b = q * T // XQ, (q + 1) * T // XQ
                sp.dma_start(x_sb[:, a:b, :], xt[:, a:b, :]).then_inc(x_in[q], 16)
            for t in range(2):
                sp.dma_start(adj_t[:, t, :], adj[t * P:(t + 1) * P, :]).then_inc(adj_in[t], 16)
            with sp.Fori(0, T // 2) as i:
                for b in range(2):
                    wait_reg(sp, "sp", hrow_ok, 2 * i + b + 3)
                    sp.dma_start(h_rows[bass.ds((2 * i + b) * P, P), :], h_row[:, b, :]).then_inc(h_st[b], 16)
                    wait_reg(sp, "sp", rrow_ok, 2 * i + b + 3)
                    sp.dma_start(r_rows[bass.ds((2 * i + b) * P, P), :], r_row[:, b, :]).then_inc(r_st[b], 16)
            for b in range(2):
                sp.wait_ge(r_st[b], 16 * (T // 2) + 16)

            def load_r(t, b, n):
                wait_reg(sp, "sp", o_ok, t + 1)
                sp.dma_start(r_in[:, b, :], r_rows[bass.ds(t * P, P), :]).then_inc(r_ld[b], 16)

            def load_adj(t, b):
                wait_reg(sp, "sp", segs_done, t + 1)
                wait_reg(sp, "sp", count_ok, t + 1)
                sp.dma_start(adj_t[:, b, :], adj[bass.ds((t + 2) * P, P), :]).then_inc(adj_in[b], 16)

            def store_o(t, b):
                wait_reg(sp, "sp", o_ok, t + 3)
                sp.dma_start(out[bass.ds(t * P, P), :], o_buf[:, b, :]).then_inc(o_st[b], 16)

            load_r(0, 0, 0)
            load_adj(0, 0)
            with sp.Fori(0, T // 2 - 2) as i:
                for b in range(2):
                    t = 2 * i + 1 + b
                    load_r(t, 1 - b, 0)
                    load_adj(t, 1 - b)
                    store_o(t - 1, b)
            for t in range(T - 3, T):
                load_r(t, t % 2, 0)
                if t + 2 < T:
                    load_adj(t, t % 2)
                store_o(t - 1, (t - 1) % 2)
            store_o(T - 1, (T - 1) % 2)
            for b in range(2):
                sp.wait_ge(o_st[b], 16 * (T // 2) + 16)

            sp.wait_ge(todo_ok, 1)
            flagged = sp.value_load(total[0:1, 0:1], min_val=0, max_val=T)
            with sp.If(flagged > 0):
                with sp.Fori(0, T) as t:
                    flag = sp.value_load(todo[0:1, t, 0:1], min_val=0, max_val=1)
                    nth = sp.value_load(todo[0:1, t, 1:2], min_val=0, max_val=T)
                    with sp.If(flag > 0):
                        wait_reg(sp, "sp", sl_free, nth * NCH + 1)
                        sp.dma_start(r_in[:, 0, :], r_rows[bass.ds(t * P, P), :]).then_inc(sl_r, 16)
                        with sp.Fori(0, NCH) as i:
                            wait_reg(sp, "sp", sl_free, nth * NCH + i + 1)
                            sp.dma_start(slots[:, 0:CHUNK, :],
                                         h_rows[bass.ds(i * CHUNK, CHUNK), :].partition_broadcast(P)).then_inc(sl_h, 16)
                            sp.dma_start(v_in[:, :], adj[bass.ds(t * P, P), bass.ds(i * CHUNK, CHUNK)]).then_inc(sl_v, 16)
                        wait_reg(sp, "sp", sl_o, nth + 1)
                        sp.dma_start(out[bass.ds(t * P, P), :], o_buf[:, 0, :]).then_inc(sl_st, 16)
                        wait_reg(sp, "sp", sl_st, 16 * nth + 32)

        @block.gpsimd
        def _(pool):
            nc.gpsimd.memset(ident[:, :], 0.0).then_inc(base_ok, 1)
            nc.gpsimd.memset(gath[:, used[0]:ROWS * C], 0.0).then_inc(consts, 1)
            nc.gpsimd.memset(ones[:, :], 1.0).then_inc(consts, 1)
            pool.wait_ge(base_ok, 1)
            nc.gpsimd.affine_select(out=ident[:, :], in_=ident[:, :], compare_op=ALU.not_equal, fill=1.0,
                                    base=0, pattern=[[-1, P]], channel_multiplier=1).then_inc(consts, 1)
            nc.gpsimd.iota(seg_i[:, :, :], [[SEG, NSEG], [0, 8]], base=CODE, channel_multiplier=0).then_inc(base_ok, 1)
            nc.gpsimd.iota(row_i[:, :], [[0, 1]], base=0, channel_multiplier=1).then_inc(base_ok, 1)
            for b in range(2):
                pool.wait_ge(h_st[b], 16 * (T // 2) + 16)
                pool.wait_ge(r_st[b], 16 * (T // 2) + 16)

            def gather(b, s):
                pool.indirect_dma_start(slots[:, row(b, s), :], None, h_rows[:, :],
                                        bass.IndirectOffsetOnAxis(ap=idx[:, b, s:s + 1], axis=0)
                                        ).then_inc(rows_in[b][s // GS], 16)

            def gather_tile(t, b):
                wait_reg(pool, "pool", list_ok, t + 1)
                longest = pool.value_load(plan[0:1, b, 0:1], min_val=0, max_val=SLOTS)
                for s in range(SLOTS):
                    if s < FIRM:
                        if s % GS == 0:
                            wait_reg(pool, "pool", sum_ok, NG * t + s // GS + 1)
                        gather(b, s)
                    else:
                        with pool.If(longest > s):
                            if s % GS == 0:
                                wait_reg(pool, "pool", sum_ok, NG * t + 2 * NG)
                            gather(b, s)

            with pool.Fori(0, T // 2) as i:
                for b in range(2):
                    gather_tile(2 * i + b, b)

        @block.scalar
        def _(act):
            act.wait_ge(var_ok, 1)
            nc.scalar.activation(rstd[:, :], mom[:, 1, :], ACT.Sqrt).then_inc(std_ok, 1)
            act.wait_ge(norm_ok, 1)

            def norm(t, b):
                wait_reg(act, "act", tr_ok, t + 1)
                nc.scalar.activation(hn[:, b, :], x_sb[:, t, :], ACT.Relu, scale=rstd[:, bass.ds(t, 1)],
                                     bias=nmr[:, bass.ds(t, 1)]).then_inc(hn_ok, 1)

            norm(0, 0)
            norm(1, 1)

            def evacuate(t, b, i):
                wait_reg(act, "act", mm_ok, t + 3)
                wait_reg(act, "act", h_st[b], 16 * i + 16)
                nc.scalar.activation(h_row[:, b, :], p_a[b][:, 0:C], ACT.Copy).then_inc(hrow_ok, 1)

            with act.Fori(0, T // 2 - 1) as i:
                for b in range(2):
                    norm(2 * i + b + 2, b)
                    evacuate(2 * i + b, b, i)
            evacuate(T - 2, 0, T // 2 - 1)
            evacuate(T - 1, 1, T // 2 - 1)

            def count(t, b, loads):
                wait_reg(act, "act", adj_in[b], loads)
                wait_reg(act, "act", kept_ok, t + 1)
                for q in range(NCNT):
                    act.drain()
                    nc.scalar.activation(sgn[:, :], adj_t[:, b, q * CNT:(q + 1) * CNT], ACT.Relu)
                    act.drain()
                    last = nc.scalar.activation(sgn[:, :], sgn[:, :], ACT.Sign,
                                                accum_out=npos[:, b, q:q + 1])
                last.then_inc(count_ok, 1)

            def score_edges(t, b):
                wait_reg(act, "act", v_ok, t + 1)
                s0 = score0[:, b, :].rearrange("p (s h) -> p s h", h=H)
                for h in range(H):
                    last = nc.scalar.activation(s0[:, :, h], vlist[:, b, :].bitcast(F32), ACT.Identity,
                                                scale=we_row[:, h:h + 1], bias=s_src[:, t, h:h + 1])
                last.then_inc(score0_ok, 1)

            def exps(t, b):
                wait_reg(act, "act", z_ok, t + 1)
                wait_reg(act, "act", sum_ok, NG * t + 2 * NG)
                nc.scalar.activation(cells[:, b * SHORT * H:(b + 1) * SHORT * H, D], z[:, 0:SHORT * H], ACT.Exp)
                nc.scalar.activation(cells[:, 2 * SHORT * H:, D], z[:, SHORT * H:], ACT.Exp).then_inc(p_ok, 1)

            count(0, 0, 16)
            score_edges(0, 0)
            with act.Fori(0, T // 2 - 1) as i:
                for b in range(2):
                    count(2 * i + b + 1, 1 - b, 16 * (i + b) + 16)
                    score_edges(2 * i + b + 1, 1 - b)
                    exps(2 * i + b, b)
            count(T - 1, 1, 16 * (T // 2))
            score_edges(T - 1, 1)
            exps(T - 2, 0)
            exps(T - 1, 1)

            act.wait_ge(todo_ok, 1)
            flagged = act.value_load(total[0:1, 0:1], min_val=0, max_val=T)
            with act.If(flagged > 0):
                with act.Fori(0, T) as t:
                    flag = act.value_load(todo[0:1, t, 0:1], min_val=0, max_val=1)
                    nth = act.value_load(todo[0:1, t, 1:2], min_val=0, max_val=T)
                    with act.If(flag > 0):
                        with act.Fori(0, NCH) as i:
                            wait_reg(act, "act", sl_z, nth * NCH + i + 1)
                            nc.scalar.activation(cells[:, 0:CHUNK * H, D], score0[:, 0, :], ACT.Exp)
                            nc.scalar.activation(corr[:, :], dmax[:, :], ACT.Exp).then_inc(sl_p, 1)

        @block.tensor
        def _(pe):
            pe.wait_ge(consts, 3)
            pe.wait_ge(w_in, 16 * (5 + 2 * KC))
            n = 0
            for nat in (w_nat, wr_nat):
                for c in range(KC):
                    for k in range(KC):
                        if n >= 2:
                            pe.wait_ge(wtr_used, n - 1)
                        nc.tensor.transpose(p_tr[n % 2][:, 0:P], nat[:, c, k * P:(k + 1) * P],
                                            ident[:, :]).then_inc(wtr_ok, 1)
                        n += 1
            pe.wait_ge(diag_ok, 1)
            for k in range(KC):
                for c in range(KC):
                    last = nc.tensor.matmul(p_b[k][:, 0:2 * H], w_nat[:, c, k * P:(k + 1) * P], a_diag[:, c, :],
                                            start=(c == 0), stop=(c == KC - 1))
                last.then_inc(wtr_ok, 1)
            pe.wait_ge(wtr_used, n + KC)

            def tr(t, b):
                wait_reg(pe, "pe", hn_ok, t + 1)
                wait_reg(pe, "pe", ht_ok, t + 1)
                for k in range(KC):
                    last = nc.tensor.transpose(p_tr[b][:, k * P:(k + 1) * P], hn[:, b, k * P:(k + 1) * P], ident[:, :])
                last.then_inc(tr_ok, 1)

            tr(0, 0)

            def project(t, b):
                wait_reg(pe, "pe", ht_ok, t + 3)
                wait_reg(pe, "pe", hrow_ok, t + 1)
                wait_reg(pe, "pe", rrow_ok, t + 1)
                for k in range(KC):
                    nc.tensor.matmul(p_a[b][:, :], h_t[:, b, k * P:(k + 1) * P], w_t[:, k, :],
                                     start=(k == 0), stop=(k == KC - 1))
                for k in range(KC):
                    nc.tensor.matmul(p_b[b][:, :], h_t[:, b, k * P:(k + 1) * P], wr_t[:, k, :],
                                     start=(k == 0), stop=False)
                last = nc.tensor.matmul(p_b[b][:, :], ones[0:1, :], bias_row[0:1, :], start=False, stop=True)
                last.then_inc(mm_ok, 1)

            with pe.Fori(0, T // 2 - 1) as i:
                for b in range(2):
                    tr(2 * i + b + 1, 1 - b)
                    project(2 * i + b, b)
            tr(T - 1, 1)
            project(T - 2, 0)
            project(T - 1, 1)

            def turn(t):
                wait_reg(pe, "pe", kept_ok, t + 3)
                nc.tensor.transpose(p_st[0:1, 0:P], kept[:, 0:1], ident[:, :])
                nc.tensor.transpose(p_st[0:1, P:2 * P], kept[:, 1:2], ident[:, :]).then_inc(worst_tr, 1)

            def part(t, b, g, stop, n):
                wait_reg(pe, "pe", w_ok, NG * t + g + 1)
                for s in range(g * GS, g * GS + GS):
                    last = nc.tensor.matmul(p_a[b][:, :], ident[:, :], slots[:, row(b, s), :],
                                            start=(s == 0), stop=(stop and s == g * GS + GS - 1))
                last.then_inc(sum_ok, n)

            def sums(t, b):
                wait_reg(pe, "pe", list_ok, t + 1)
                longest = pe.value_load(plan[0:1, b, 0:1], min_val=0, max_val=SLOTS)
                wait_reg(pe, "pe", done, t + 1)
                for g in range(NS - 1):
                    part(t, b, g, False, 1)
                with pe.If(longest > SHORT):
                    part(t, b, NS - 1, False, 1)
                    for g in range(NS, NG):
                        part(t, b, g, g == NG - 1, 1)
                with pe.Else():
                    part(t, b, NS - 1, True, 1 + NG - NS)

            turn(0)
            with pe.Fori(0, T // 2 - 1) as i:
                for b in range(2):
                    turn(2 * i + b + 1)
                    sums(2 * i + b, b)
            turn(T - 1)
            sums(T - 2, 0)
            sums(T - 1, 1)

            pe.wait_ge(todo_ok, 1)
            flagged = pe.value_load(total[0:1, 0:1], min_val=0, max_val=T)
            with pe.If(flagged > 0):
                with pe.Fori(0, T) as t:
                    flag = pe.value_load(todo[0:1, t, 0:1], min_val=0, max_val=1)
                    nth = pe.value_load(todo[0:1, t, 1:2], min_val=0, max_val=T)
                    with pe.If(flag > 0):
                        with pe.Fori(0, NCH) as i:
                            wait_reg(pe, "pe", sl_p, nth * NCH + i + 1)
                            wait_reg(pe, "pe", sl_w, nth * NCH + i + 1)
                            for s in range(CHUNK):
                                last = nc.tensor.matmul(p_a[0][:, 0:C], ident[:, :], slots[:, s, :],
                                                        start=(s == 0), stop=(s == CHUNK - 1))
                            last.then_inc(sl_sum, 1)

        @block.vector
        def _(v):
            V = nc.vector

            def bc(ap, shape, axis):
                return ap.unsqueeze(axis).broadcast_to(shape)

            for sm, n in ((tr_ok, 2), (ht_ok, 2), (mm_ok, 2), (hrow_ok, 2), (rrow_ok, 2), (kept_ok, 2),
                          (done, 2), (o_ok, 2), (sum_ok, 2 * NG), (sl_free, 1), (sl_st, 16),
                          *((st, 16) for st in (*h_st, *r_st, *o_st))):
                v.sem_inc(sm, n)
            V.memset(a_diag[:, :, :], 0.0)
            V.memset(cum[:, :, :], 0.0)
            V.memset(z[:, :], 0.0)
            V.memset(ords[:, :], 0.0)
            v.wait_ge(w_in, 16 * (5 + 2 * KC))
            v.drain()
            for n in range(2):
                for c in range(KC):
                    for q in range(HC):
                        r = slice(q * D, (q + 1) * D)
                        last = V.tensor_copy(a_diag[r, c, n * H + c * HC + q:n * H + c * HC + q + 1],
                                             a_col[r, n, c:c + 1])
            last.then_inc(diag_ok, 1)
            heads = w_t[:, :, 0:C].rearrange("p k (h e) -> p k h e", e=E)
            n = 0
            for is_r in range(2):
                for c in range(KC):
                    for k in range(KC):
                        v.wait_ge(wtr_ok, n + 1)
                        if is_r:
                            V.tensor_copy(wr_t[:, k, c * P:(c + 1) * P], p_tr[n % 2][:, 0:P]).then_inc(wtr_used, 1)
                        else:
                            V.tensor_copy(heads[:, k, c * HC:(c + 1) * HC, 0:D],
                                          p_tr[n % 2][:, 0:P].rearrange("p (h d) -> p h d", d=D)).then_inc(wtr_used, 1)
                        n += 1
            for k in range(KC):
                v.wait_ge(wtr_ok, n + k + 1)
                V.tensor_copy(wr_t[:, k, IN:RS], p_b[k][:, 0:H])
                V.tensor_copy(heads[:, k, :, D], p_b[k][:, H:2 * H]).then_inc(wtr_used, 1)

            for q in range(XQ):
                v.wait_ge(x_in[q], 16)
                with v.Fori(q * T // XQ, (q + 1) * T // XQ) as t:
                    V.bn_stats(stats[:, t, :], x_sb[:, t, :])
            v.drain()
            V.tensor_tensor(mom[:, 0, :], stats[:, :, 1], stats[:, :, 4], ALU.add)
            V.tensor_tensor(mom[:, 1, :], stats[:, :, 2], stats[:, :, 5], ALU.add)
            V.tensor_tensor(mom[:, 2, :], stats[:, :, 1], stats[:, :, 4], ALU.subtract)
            v.drain()
            V.tensor_tensor(mom[:, 2, :], mom[:, 2, :], mom[:, 2, :], ALU.mult)
            V.tensor_scalar(mom[:, 0, :], mom[:, 0, :], 0.5, None, ALU.mult)
            V.tensor_scalar(mom[:, 1, :], mom[:, 1, :], 1.0 / IN, EPS, ALU.mult, ALU.add)
            v.drain()
            V.scalar_tensor_tensor(mom[:, 1, :], mom[:, 2, :], 0.25, mom[:, 1, :], ALU.mult, ALU.add).then_inc(var_ok, 1)
            v.wait_ge(std_ok, 1)
            V.reciprocal(rstd[:, :], rstd[:, :])
            v.drain()
            V.scalar_tensor_tensor(nmr[:, :], mom[:, 0, :], -1.0, rstd[:, :], ALU.mult, ALU.mult).then_inc(norm_ok, 1)

            v.wait_ge(base_ok, 3)
            V.tensor_copy(seg_base[:, :], seg_i[:, :, :].rearrange("p n k -> p (n k)"))
            V.tensor_copy(row_id[:, :], row_i[:, :])

            def copy_ht(t, b):
                wait_reg(v, "dve", tr_ok, t + 3)
                wait_reg(v, "dve", mm_ok, t + 1)
                V.tensor_copy(h_t[:, b, :], p_tr[b][:, :]).then_inc(ht_ok, 1)

            def residual(t, b, i):
                wait_reg(v, "dve", mm_ok, t + 3)
                wait_reg(v, "dve", r_st[b], 16 * i + 16)
                V.tensor_copy(s_src[:, bass.ds(t, 1), :].squeeze(1), p_b[b][:, IN:RS])
                V.tensor_tensor(r_row[:, b, :], p_b[b][:, 0:IN], x_sb[:, bass.ds(t, 1), :].squeeze(1),
                                ALU.add).then_inc(rrow_ok, 1)

            copy_ht(0, 0)
            with v.Fori(0, T // 2 - 1) as i:
                for b in range(2):
                    copy_ht(2 * i + b + 1, 1 - b)
                    residual(2 * i + b, b, i)
            copy_ht(T - 1, 1)
            residual(T - 2, 0, T // 2 - 1)
            residual(T - 1, 1, T // 2 - 1)

            def f(ap):
                return ap.bitcast(F32)

            def pack(t, b, loads):
                wait_reg(v, "dve", adj_in[b], loads)
                for n in range(NSEG):
                    V.max(top_v[:, 8 * n:8 * n + 8], adj_t[:, b, n * SEG:(n + 1) * SEG])
                v.drain()
                for n in range(NSEG):
                    last = V.max_index(top_j[:, 8 * n:8 * n + 8], top_v[:, 8 * n:8 * n + 8],
                                       adj_t[:, b, n * SEG:(n + 1) * SEG])
                last.then_inc(segs_done, 1)
                v.drain()
                V.tensor_tensor(col, top_j[:, :], seg_base[:, :], ALU.add)
                V.tensor_scalar(vpos[:, :], top_v[:, :], 0.0, None, ALU.max)
                V.tensor_scalar(junk, top_v[:, :], 0.0, 0.0, ALU.is_gt, ALU.add, accum_out=kept[:, 0:1])
                v.drain()
                V.scalar_tensor_tensor(code[:, :], vpos[:, :], 0.0, col, ALU.is_gt, ALU.mult)
                wait_reg(v, "dve", count_ok, t + 1)
                V.tensor_reduce(kept[:, 1:2], npos[:, b, :], axis=AX.X, op=ALU.add)
                v.drain()
                V.tensor_scalar(key_hi[:, :], code[:, :], 16, None, ALU.logical_shift_left)
                V.tensor_tensor(kept[:, 1:2], kept[:, 1:2], kept[:, 0:1], ALU.not_equal)
                v.drain()
                V.scalar_tensor_tensor(kept[:, 1:2], kept[:, 0:1], float(SLOTS), kept[:, 1:2],
                                       ALU.is_gt, ALU.max).then_inc(kept_ok, 1)
                bits = vpos[:, :].bitcast(U32)
                V.scalar_tensor_tensor(key_lo[:, :], bits, 0xFFFF, key_hi[:, :], ALU.bitwise_and, ALU.bitwise_or)
                v.drain()
                V.scalar_tensor_tensor(key_hi[:, :], bits, 16, key_hi[:, :], ALU.logical_shift_right, ALU.bitwise_or)
                v.drain()
                def rank(r0, r1):
                    for r in range(r0, r1):
                        s = slice(8 * r, 8 * r + 8)
                        for lst, key in ((list_hi, key_hi), (list_lo, key_lo)):
                            V.max(f(lst[:, s]), f(key[:, :]))
                        v.drain()
                        if r < SLOTS // 8 - 1:
                            for lst, key in ((list_hi, key_hi), (list_lo, key_lo)):
                                V.match_replace(f(key[:, :]), f(lst[:, s]), f(key[:, :]), 0.0)
                            v.drain()

                rank(0, 4)
                wait_reg(v, "dve", worst_tr, t + 1)
                V.tensor_reduce(worst[:, :], p_st[0:1, :].rearrange("p (a q) -> p a q", q=P), axis=AX.X, op=ALU.max)
                v.drain()
                V.tensor_copy(flags[0:1, bass.ds(t, 1)], worst[:, 1:2])
                V.tensor_scalar(cut[:, 0:1], worst[:, 0:1], float(SLOTS), None, ALU.min)
                v.drain()
                for n, g in enumerate((NS - 1, NS)):
                    V.tensor_scalar(cut[:, n + 1:n + 2], cut[:, 0:1], float(-GS * g), FIRM % GS if n == 0 else 0.0,
                                    ALU.add, ALU.max)
                v.drain()
                V.tensor_scalar(cut[:, 1:], cut[:, 1:], float(GS), 16.0, ALU.min, ALU.mult)
                v.drain()
                V.tensor_tensor(cum[:, b, 1:], cum[:, b, 1:], cut[:, 1:], ALU.add)
                V.tensor_copy(cum[:, b, 0:1], cut[:, 0:1])
                v.drain()
                V.tensor_copy(plan[:, b, :], cum[:, b, :]).then_inc(plan_self, 1)
                rank(4, SHORT // 8)
                wait_reg(v, "dve", plan_self, t + 1)
                longest = v.value_load(plan[0:1, b, 0:1], min_val=0, max_val=SLOTS)
                with v.If(longest > SHORT):
                    rank(SHORT // 8, SLOTS // 8)
                with v.Else():
                    V.memset(list_hi[:, SHORT:], 0)
                    V.memset(list_lo[:, SHORT:], 0)
                v.drain()
                V.tensor_scalar(vhi[:, :], list_hi[:, :], 0xFFFF, 16, ALU.bitwise_and, ALU.logical_shift_left)
                V.tensor_scalar(nb[:, :], list_hi[:, :], 16, CODE - 1, ALU.logical_shift_right, ALU.bitwise_and)
                V.tensor_scalar(own[:, :], f(list_hi[:, :]), 0.0, row_id[:, 0:1], ALU.is_equal, ALU.mult)
                V.tensor_scalar(pen[:, b, :], f(list_hi[:, :]), 0.0, PAD, ALU.is_equal, ALU.mult)
                v.drain()
                V.scalar_tensor_tensor(vlist[:, b, :], list_lo[:, :], 0xFFFF, vhi[:, :],
                                       ALU.bitwise_and, ALU.bitwise_or).then_inc(v_ok, 1)
                V.tensor_tensor(idx[:, b, :], nb[:, :], own[:, :], ALU.add).then_inc(list_ok, 1)
                V.tensor_scalar(row_id[:, :], row_id[:, :], float(P), None, ALU.add)

            def score(t, b, n):
                zz = z[:, 0:n * H]
                z3 = zz.rearrange("p (s h) -> p s h", h=H)
                for s0, s1 in ((0, SHORT), (SHORT, n))[:1 + (n > SHORT)]:
                    V.tensor_tensor(z[:, s0 * H:s1 * H], score0[:, b, s0 * H:s1 * H],
                                    cells[:, row(b, s0) * H:row(b, s1 - 1) * H + H, D], ALU.add)
                v.drain()
                V.tensor_tensor(z3, z3, bc(pen[:, b, 0:n], [P, n, H], 2), ALU.add)
                v.drain()
                V.scalar_tensor_tensor(zz, zz, ALPHA, zz, ALU.mult, ALU.max)
                v.drain()
                V.tensor_reduce(gmax[:, :], zz.rearrange("p (s h) -> p h s", h=H), axis=AX.X, op=ALU.max)
                v.drain()
                V.tensor_scalar(gmax[:, :], gmax[:, :], FLOOR, None, ALU.max)
                v.drain()
                V.tensor_tensor(z3, z3, bc(gmax[:, :], [P, n, H], 1), ALU.subtract).then_inc(z_ok, 1)

            def weigh(b, g):
                a = slice(row(b, g * GS) * H, row(b, g * GS) * H + GS * H)
                V.tensor_tensor(cells[:, a, 0:D], cells[:, a, 0:D],
                                cells[:, a, D:E].broadcast_to([P, GS * H, D]), ALU.mult).then_inc(w_ok, 1)

            def attend(t, b, i, prev):
                longest, upto_a, upto_b = [v.value_load(plan[0:1, b, n:n + 1], min_val=lo, max_val=hi) for n, lo, hi in
                                           ((0, 0, SLOTS), (1, 16, 16 * GS * T), (2, 0, 16 * GS * T))]
                wait_reg(v, "dve", score0_ok, t + 1)
                for g in range(NS - 1):
                    wait_reg(v, "dve", rows_in[b][g], (i + 1) * 16 * GS)
                wait_reg(v, "dve", rows_in[b][NS - 1], upto_a)
                with v.If(longest > SHORT):
                    wait_reg(v, "dve", rows_in[b][NS], upto_b)
                    score(t, b, SLOTS)
                with v.Else():
                    score(t, b, SHORT)
                if prev is not None:
                    settle(*prev)
                wait_reg(v, "dve", p_ok, t + 1)
                for g in range(NS):
                    weigh(b, g)
                with v.If(longest > SHORT):
                    for g in range(NS, NG):
                        weigh(b, g)
                with v.Else():
                    v.drain().then_inc(w_ok, NG - NS)

            def settle(t, b, i):
                wait_reg(v, "dve", sum_ok, NG * t + 3 * NG)
                wait_reg(v, "dve", r_ld[b], 16 * i + 16)
                wait_reg(v, "dve", o_st[b], 16 * i + 16)
                finish(b, p_a[b][:, :], o_ok, done)

            def finish(b, sums, stored, freed):
                a3 = sums.rearrange("p (h e) -> p h e", e=E)
                V.reciprocal(rden[:, :], a3[:, :, D])
                v.drain()
                prod = V.tensor_tensor(o_buf[:, b, :].rearrange("p (h d) -> p h d", d=D), a3[:, :, 0:D],
                                       bc(rden[:, :], [P, H, D], 2), ALU.mult)
                if freed is not None:
                    prod.then_inc(freed, 1)
                v.drain()
                V.tensor_tensor(o_buf[:, b, :], o_buf[:, b, :], r_in[:, b, :], ALU.add).then_inc(stored, 1)

            v.drain()
            pack(0, 0, 16)
            pack(1, 1, 16)
            attend(0, 0, 0, None)
            with v.Fori(0, T // 2 - 1) as i:
                pack(2 * i + 2, 0, 16 * i + 32)
                attend(2 * i + 1, 1, i, (2 * i, 0, i))
                pack(2 * i + 3, 1, 16 * i + 32)
                attend(2 * i + 2, 0, i + 1, (2 * i + 1, 1, i))
            attend(T - 1, 1, T // 2 - 1, (T - 2, 0, T // 2 - 1))
            settle(T - 1, 1, T // 2 - 1)

            v.drain()
            V.tensor_tensor_scan(ords[0:1, 1:], flags[0:1, :], flags[0:1, :], 0.0, ALU.add, ALU.bypass)
            V.tensor_copy(todo[0:1, :, 0], flags[0:1, :])
            v.drain()
            V.tensor_copy(total[0:1, :], ords[0:1, T:])
            v.drain()
            V.tensor_copy(todo[0:1, :, 1], ords[0:1, 0:T]).then_inc(todo_ok, 1)
            v.wait_ge(todo_ok, 1)
            flagged = v.value_load(total[0:1, 0:1], min_val=0, max_val=T)
            with v.If(flagged > 0):
                with v.Fori(0, T) as t:
                    flag = v.value_load(todo[0:1, t, 0:1], min_val=0, max_val=1)
                    nth = v.value_load(todo[0:1, t, 1:2], min_val=0, max_val=T)
                    with v.If(flag > 0):
                        V.memset(m[:, 0, :], FLOOR)
                        V.memset(acc, 0.0)
                        with v.Fori(0, NCH) as i:
                            n = nth * NCH + i
                            s3 = [P, CHUNK, H]
                            s0 = score0[:, 0, :].rearrange("p (s h) -> p s h", h=H)
                            a3 = acc.rearrange("p (h e) -> p h e", e=E)
                            wait_reg(v, "dve", sl_v, 16 * n + 16)
                            V.tensor_tensor(s0, bc(v_in[:, :], s3, 2), bc(we_row[:, :], s3, 1), ALU.mult)
                            V.tensor_scalar(pen[:, 0, :], v_in[:, :], 0.0, PAD, ALU.is_le, ALU.mult)
                            v.drain()
                            V.tensor_tensor(s0, s0, s_src[:, bass.ds(t, 1), :].broadcast_to(s3), ALU.add)
                            wait_reg(v, "dve", sl_h, 16 * n + 16)
                            v.drain()
                            V.tensor_tensor(score0[:, 0, :], score0[:, 0, :], cells[:, 0:CHUNK * H, D], ALU.add)
                            v.drain()
                            V.tensor_tensor(s0, s0, bc(pen[:, 0, :], s3, 2), ALU.add)
                            v.drain()
                            V.scalar_tensor_tensor(s0, s0, ALPHA, s0, ALU.mult, ALU.max)
                            v.drain()
                            V.tensor_reduce(gmax[:, :], s0.rearrange("p s h -> p h s"), axis=AX.X, op=ALU.max)
                            v.drain()
                            V.tensor_tensor(m[:, 1, :], gmax[:, :], m[:, 0, :], ALU.max)
                            v.drain()
                            V.tensor_tensor(dmax[:, :], m[:, 0, :], m[:, 1, :], ALU.subtract)
                            v.drain()
                            V.tensor_copy(m[:, 0, :], m[:, 1, :])
                            V.tensor_tensor(s0, s0, bc(m[:, 1, :], s3, 1), ALU.subtract).then_inc(sl_z, 1)
                            wait_reg(v, "dve", sl_p, n + 1)
                            V.tensor_tensor(cells[:, 0:CHUNK * H, 0:D], cells[:, 0:CHUNK * H, 0:D],
                                            cells[:, 0:CHUNK * H, D:E].broadcast_to([P, CHUNK * H, D]), ALU.mult).then_inc(sl_w, 1)
                            V.tensor_tensor(a3, a3, bc(corr[:, :], [P, H, E], 2), ALU.mult)
                            wait_reg(v, "dve", sl_sum, n + 1)
                            v.drain()
                            V.tensor_tensor(acc, acc, p_a[0][:, 0:C], ALU.add).then_inc(sl_free, 1)
                        v.drain()
                        wait_reg(v, "dve", sl_r, 16 * nth + 16)
                        wait_reg(v, "dve", sl_st, 16 * nth + 16)
                        finish(0, acc, sl_o, None)
                        v.drain()


_INS = ["x", "adj", "L0_gnn_W", "L0_gnn_We", "L0_gnn_be", "L0_gnn_a_src", "L0_gnn_a_dst", "L0_gnn_Wr", "L0_gnn_br"]


def kernel(**inputs):
    import numpy as _np
    import concourse.bacc as _bacc
    from concourse import mybir as _mybir
    from concourse.bass_utils import run_bass_kernel_spmd as _run

    nc = _bacc.Bacc("TRN2", target_bir_lowering=False, num_devices=1)
    arrays, args = {}, []
    for name in _INS:
        a = _np.ascontiguousarray(inputs[name])
        arrays[f"in_{name}_dram"] = a
        args.append(nc.dram_tensor(f"in_{name}_dram", a.shape, _mybir.dt.from_np(a.dtype), kind="ExternalInput").ap())
    args.append(nc.dram_tensor("out_0_dram", inputs["x"].shape, _mybir.dt.float32, kind="ExternalOutput").ap())
    build(nc, *args)
    r = _run(nc, [arrays], core_ids=[0])
    return r.results[0]["out_0_dram"]
```

```python
import concourse.bass as bass
from concourse import mybir
from contextlib import ExitStack

F32 = mybir.dt.float32
BF16 = mybir.dt.bfloat16
U32 = mybir.dt.uint32
I32 = mybir.dt.int32
ALU = mybir.AluOpType
ACT = mybir.ActivationFunctionType
AX = mybir.AxisListType

P = 128
ALPHA = 0.2
EPS = 1e-5
SEG = 256
SLOTS = 64
SHORT = 48
MID = 56
FIRM = 40
GS = 16
NG = SLOTS // GS
NS = SHORT // GS
LEAD = 4
SHARE = 12
STEP = 4
ROWS = 2 * SHORT + SLOTS - SHORT
CODE = 8192
PAD = -1.5e38
FLOOR = -2.5e37
CHUNK = 64


def build(nc, x, adj, W, We, be, a_src, a_dst, Wr, br, out):
    N, IN = x.shape
    H, D = a_src.shape
    E = D + 1
    C = H * E
    CS = C + H
    T = N // P
    NSEG = N // SEG
    KC = IN // P
    HC = H // KC
    XQ = 4
    TQ = T // XQ
    IQ = TQ // 4
    AP = T // 8
    PIECE = N // AP
    CNT = 512
    NCNT = N // CNT
    SEG_I = NSEG // IQ
    NCH = N // CHUNK

    h_rows = nc.dram_tensor("h_rows", (N + P, C), F32, kind="Internal").ap()

    ctx = ExitStack()
    with ctx:
        def sb(name, shape, dt=F32):
            return ctx.enter_context(nc.sbuf_tensor(name, shape, dt))

        def ps(name, shape):
            return ctx.enter_context(nc.psum_tensor(name, shape, F32))

        def sem(name):
            return ctx.enter_context(nc.semaphore(name))

        ident = sb("ident", [P, P])
        ones = sb("ones", [1, P])
        br_row = sb("br_row", [1, IN])
        wr_t = sb("wr_t", [P, KC, IN])
        a_col = sb("a_col", [P, 2, KC])
        a_diag = sb("a_diag", [P, KC, 2 * H])
        we_row = sb("we_row", [P, H])
        s_src = sb("s_src", [P, T, H])

        gath = sb("gath", [P, ROWS * C])

        used = [T * IN]

        def before(*shape):
            n = 1
            for k in shape:
                n *= k
            used[0] += n
            flat = gath[:, used[0] - n:used[0]]
            return flat.rearrange("p (a b) -> p a b", a=shape[0]) if len(shape) == 2 else flat

        w_nat, wr_nat = before(KC, IN), before(KC, IN)
        w_t = before(KC, CS)
        stats = before(T, 6)
        hn, h_t = before(4, IN), before(4, IN)
        h_row = before(4, C)
        mom = before(3, T)
        rstd, nmr = sb("rstd", [P, T]), sb("nmr", [P, T])
        seg_i = before(NSEG, 8).bitcast(U32)
        be_row = before(H)
        adj_t = sb("adj_t", [P, 2, N])
        seg_base = sb("seg_base", [P, NSEG * 8], U32)
        row_i = sb("row_i", [P, 1], I32)
        row_id = sb("row_id", [P, 1])
        top_v = sb("top_v", [P, NSEG * 8])
        top_j = sb("top_j", [P, NSEG * 8], U32)
        key_hi = sb("key_hi", [P, NSEG * 8], U32)
        key_lo = sb("key_lo", [P, NSEG * 8], U32)
        code = top_j
        junk = key_hi[:, :].bitcast(F32)
        list_hi = sb("list_hi", [P, SLOTS], U32)
        list_lo = sb("list_lo", [P, SLOTS], U32)
        nb, vhi = key_hi[:, 0:SLOTS], key_hi[:, SLOTS:2 * SLOTS]
        own = key_lo[:, 0:SLOTS].bitcast(F32)
        pen = sb("pen", [P, 2, SLOTS])
        vlist = sb("vlist", [P, 2, SLOTS], U32)
        idx = sb("idx", [P, 2, SLOTS], U32)
        score0 = sb("score0", [P, 2, SLOTS * H])
        sgn = sb("sgn", [P, CNT], BF16)
        npos = sb("npos", [P, 2, NCNT])
        kept = sb("kept", [P, 2])
        worst = sb("worst", [1, 2])
        cut = sb("cut", [1, 3])
        cum = sb("cum", [1, 2, 3])
        plan = sb("plan", [1, 2, 3], U32)
        flags = sb("flags", [1, T])
        ords = sb("ords", [1, T + 1])
        todo = sb("todo", [1, T, 2], U32)
        total = sb("total", [1, 1], U32)
        z = sb("z", [P, SLOTS * H])
        dmax = sb("dmax", [P, H])
        corr = sb("corr", [P, H])
        gmax = sb("gmax", [P, H])
        m = sb("m", [P, 2, H])
        acc = z[:, 0:C]
        rden = sb("rden", [P, H])
        x_tile = sb("x_tile", [P, 2, IN])
        ht_in = sb("ht_in", [P, 2, IN])
        o_buf = sb("o_buf", [P, 2, IN])
        v_in = key_hi[:, 0:CHUNK].bitcast(F32)

        p_tr = [ps(f"p_tr{i}", [P, IN]) for i in range(2)]
        p_a = [ps(f"p_a{i}", [P, CS]) for i in range(2)]
        p_b = [ps(f"p_b{i}", [P, IN]) for i in range(2)]
        p_st = ps("p_st", [P, 2 * P])

        x_sb = gath[:, 0:T * IN].rearrange("p (t c) -> p t c", c=IN)
        slots = gath[:, :].rearrange("p (s c) -> p s c", c=C)
        cells = gath[:, :].rearrange("p (a e) -> p a e", e=E)

        def row(b, s):
            return b * SHORT + s if s < SHORT else SHORT + s

        w_in = sem("w_in")
        x_in = [sem(f"x_in{q}") for q in range(XQ)]
        consts = sem("consts")
        diag_ok = sem("diag_ok")
        wtr_ok = sem("wtr_ok")
        wtr_used = sem("wtr_used")
        var_ok = sem("var_ok")
        std_ok = sem("std_ok")
        norm_ok = sem("norm_ok")
        hn_ok = sem("hn_ok")
        tr_ok = sem("tr_ok")
        ht_ok = sem("ht_ok")
        mm_ok = sem("mm_ok")
        hrow_ok = sem("hrow_ok")
        pad_ok = sem("pad_ok")
        pad_st = sem("pad_st")
        h_st = [sem(f"h_st{i}") for i in range(2)]
        base_ok = sem("base_ok")
        adj_in = [sem(f"adj_in{i}") for i in range(2)]
        segs_done = sem("segs_done")
        count_ok = sem("count_ok")
        kept_ok = sem("kept_ok")
        worst_tr = sem("worst_tr")
        plan_self = sem("plan_self")
        list_ok = sem("list_ok")
        rows_in = [[sem(f"rows_in{b}_{g}") for g in range(NG)] for b in range(2)]
        z_ok = sem("z_ok")
        p_ok = sem("p_ok")
        w_ok = sem("w_ok")
        sum_ok = sem("sum_ok")
        lead_ok = sem("lead_ok")
        a_ok = sem("a_ok")
        src_ok = sem("src_ok")
        v_ok = sem("v_ok")
        score0_ok = sem("score0_ok")
        x_ld = [sem(f"x_ld{i}") for i in range(2)]
        again_ok = sem("again_ok")
        again_tr = sem("again_tr")
        ht_in_ok = sem("ht_in_ok")
        o_ok = sem("o_ok")
        o_st = [sem(f"o_st{i}") for i in range(2)]
        todo_ok = sem("todo_ok")
        sl_h = sem("sl_h")
        sl_v = sem("sl_v")
        sl_x = sem("sl_x")
        sl_again = sem("sl_again")
        sl_tr = sem("sl_tr")
        sl_ht = sem("sl_ht")
        sl_res = sem("sl_res")
        sl_z = sem("sl_z")
        sl_p = sem("sl_p")
        sl_w = sem("sl_w")
        sl_sum = sem("sl_sum")
        sl_free = sem("sl_free")
        sl_o = sem("sl_o")
        sl_st = sem("sl_st")
        passed = {k: sem(f"passed_{k}") for k in ("sp", "pool", "act", "dve", "pe")}

        def loaded(b, k):
            return 16 * k + (16 * AP if b == 0 else 16)

        def wait_reg(eng, name, sm, value):
            eng.wait_ge(sm, value)
            eng.sem_inc(passed[name], 1)

        block = ctx.enter_context(nc.Block())

        @block.sync
        def _(sp):
            for n, (dst, src) in enumerate(((w_nat, W), (wr_nat, Wr))):
                sp.dma_start(dst[:, :, :], src.rearrange("(c p) i -> p c i", p=P)).then_inc(w_in, 16)
            with nc.allow_non_contiguous_dma(reason="small vectors"):
                for n, a in enumerate((a_src, a_dst)):
                    for c in range(KC):
                        sp.dma_start(a_col[:, n, c:c + 1],
                                     a[c * HC:(c + 1) * HC, :].rearrange("h (d o) -> (h d) o", o=1)).then_inc(w_in, 16)
                sp.dma_start(we_row[:, :], We.rearrange("h o -> o h").partition_broadcast(P)).then_inc(w_in, 16)
                sp.dma_start(be_row[:, :], be.rearrange("(o h) -> o h", o=1).partition_broadcast(P)).then_inc(w_in, 16)
            sp.dma_start(br_row[0:1, :], br.rearrange("(o h) -> o h", o=1)).then_inc(w_in, 16)
            xt = x.rearrange("(t p) c -> p t c", p=P)
            for q in range(XQ):
                a, b = q * TQ, (q + 1) * TQ
                sp.dma_start(x_sb[:, a:b, :], xt[:, a:b, :]).then_inc(x_in[q], 16)
            sp.wait_ge(pad_ok, 1)
            sp.dma_start(h_rows[N:N + P, :], z[:, 0:C]).then_inc(pad_st, 16)
            def store_rows(i):
                for q in range(2):
                    pair = bass.ds((4 * i + 2 * q) * P, 2 * P)
                    wait_reg(sp, "sp", hrow_ok, 4 * i + 2 * q + 4)
                    sp.dma_start(h_rows[pair, :].rearrange("(k p) c -> p k c", p=P),
                                 h_row[:, 2 * q:2 * q + 2, :]).then_inc(h_st[q], 16)

            with sp.Fori(0, AP) as i:
                piece = bass.ds(i * PIECE, PIECE)
                sp.dma_start(adj_t[:, 0, piece], adj[0:P, piece]).then_inc(adj_in[0], 16)
                store_rows(i)
            with sp.Fori(AP, T // 4) as i:
                store_rows(i)
            sp.dma_start(adj_t[:, 1, :], adj[P:2 * P, :]).then_inc(adj_in[1], 16)

            def load_x(t, b):
                wait_reg(sp, "sp", o_ok, t + 1)
                sp.dma_start(x_tile[:, b, :], x[bass.ds(t * P, P), :]).then_inc(x_ld[b], 16)

            def load_adj(t, b):
                wait_reg(sp, "sp", segs_done, t + 1)
                wait_reg(sp, "sp", count_ok, t + 1)
                sp.dma_start(adj_t[:, b, :], adj[bass.ds((t + 2) * P, P), :]).then_inc(adj_in[b], 16)

            def store_o(t, b):
                wait_reg(sp, "sp", o_ok, t + 3)
                sp.dma_start(out[bass.ds(t * P, P), :], o_buf[:, b, :]).then_inc(o_st[b], 16)

            load_x(0, 0)
            load_adj(0, 0)
            with sp.Fori(0, T // 2 - 2) as i:
                for b in range(2):
                    t = 2 * i + 1 + b
                    load_x(t, 1 - b)
                    load_adj(t, 1 - b)
                    store_o(t - 1, b)
            for t in range(T - 3, T):
                load_x(t, t % 2)
                if t + 2 < T:
                    load_adj(t, t % 2)
                store_o(t - 1, (t - 1) % 2)
            store_o(T - 1, (T - 1) % 2)
            for b in range(2):
                sp.wait_ge(o_st[b], 16 * (T // 2) + 16)

            sp.wait_ge(todo_ok, 1)
            flagged = sp.value_load(total[0:1, 0:1], min_val=0, max_val=T)
            with sp.If(flagged > 0):
                with sp.Fori(0, T) as t:
                    flag = sp.value_load(todo[0:1, t, 0:1], min_val=0, max_val=1)
                    nth = sp.value_load(todo[0:1, t, 1:2], min_val=0, max_val=T)
                    with sp.If(flag > 0):
                        wait_reg(sp, "sp", sl_free, nth * NCH + 1)
                        sp.dma_start(x_tile[:, 0, :], x[bass.ds(t * P, P), :]).then_inc(sl_x, 16)
                        with sp.Fori(0, NCH) as i:
                            wait_reg(sp, "sp", sl_free, nth * NCH + i + 1)
                            sp.dma_start(slots[:, 0:CHUNK, :],
                                         h_rows[bass.ds(i * CHUNK, CHUNK), :].partition_broadcast(P)).then_inc(sl_h, 16)
                            sp.dma_start(v_in, adj[bass.ds(t * P, P), bass.ds(i * CHUNK, CHUNK)]).then_inc(sl_v, 16)
                        wait_reg(sp, "sp", sl_o, nth + 1)
                        sp.dma_start(out[bass.ds(t * P, P), :], o_buf[:, 0, :]).then_inc(sl_st, 16)
                        wait_reg(sp, "sp", sl_st, 16 * nth + 32)

        @block.gpsimd
        def _(pool):
            nc.gpsimd.memset(ident[:, :], 0.0).then_inc(base_ok, 1)
            nc.gpsimd.memset(ones[:, :], 1.0).then_inc(consts, 1)
            nc.gpsimd.iota(seg_i[:, :, :], [[SEG, NSEG], [0, 8]], base=CODE, channel_multiplier=0).then_inc(base_ok, 1)
            nc.gpsimd.iota(row_i[:, :], [[0, 1]], base=N, channel_multiplier=1).then_inc(base_ok, 1)
            pool.wait_ge(base_ok, 3)
            nc.gpsimd.affine_select(out=ident[:, :], in_=ident[:, :], compare_op=ALU.not_equal, fill=1.0,
                                    base=0, pattern=[[-1, P]], channel_multiplier=1).then_inc(consts, 1)
            nc.gpsimd.memset(gath[:, used[0]:ROWS * C], 0.0).then_inc(consts, 1)
            pool.wait_ge(pad_st, 16)
            for b in range(2):
                pool.wait_ge(h_st[b], 16 * (T // 4) + 16)

            def gather(b, s):
                pool.indirect_dma_start(slots[:, row(b, s), :], None, h_rows[:, :],
                                        bass.IndirectOffsetOnAxis(ap=idx[:, b, s:s + 1], axis=0)
                                        ).then_inc(rows_in[b][s // GS], 16)

            def gather_tile(t, b):
                wait_reg(pool, "pool", list_ok, t + 1)
                longest = pool.value_load(plan[0:1, b, 0:1], min_val=0, max_val=SLOTS)
                for s in range(SLOTS):
                    if s < FIRM:
                        if s % GS == 0:
                            wait_reg(pool, "pool", sum_ok, NG * t + s // GS + 1)
                        gather(b, s)
                    else:
                        with pool.If(longest > s):
                            if s % GS == 0:
                                wait_reg(pool, "pool", sum_ok, NG * t + 2 * NG)
                            gather(b, s)

            with pool.Fori(0, T // 2) as i:
                for b in range(2):
                    gather_tile(2 * i + b, b)

        @block.scalar
        def _(act):
            def count(t, b, loads):
                wait_reg(act, "act", adj_in[b], loads)
                wait_reg(act, "act", kept_ok, t + 1)
                for q in range(NCNT):
                    act.drain()
                    nc.scalar.activation(sgn[:, :], adj_t[:, b, q * CNT:(q + 1) * CNT], ACT.Relu)
                    act.drain()
                    last = nc.scalar.activation(sgn[:, :], sgn[:, :], ACT.Sign, accum_out=npos[:, b, q:q + 1])
                last.then_inc(count_ok, 1)

            def deviations(q):
                r = slice(q * TQ, (q + 1) * TQ)
                act.wait_ge(var_ok, q + 1)
                nc.scalar.activation(rstd[:, r], mom[:, 1, r], ACT.Sqrt).then_inc(std_ok, 1)

            def norm(t, b):
                nc.scalar.activation(hn[:, b, :], x_sb[:, t, :], ACT.Relu, scale=rstd[:, bass.ds(t, 1)],
                                     bias=nmr[:, bass.ds(t, 1)]).then_inc(hn_ok, 1)

            def evacuate(t, b, i):
                wait_reg(act, "act", mm_ok, t + 3)
                if b % 2 == 0:
                    wait_reg(act, "act", h_st[b // 2], 16 * i + 16)
                nc.scalar.activation(s_src[:, t, :], p_a[b % 2][:, C:CS], ACT.Copy)
                nc.scalar.activation(h_row[:, b, :], p_a[b % 2][:, 0:C], ACT.Copy).then_inc(hrow_ok, 1)

            deviations(0)
            deviations(1)
            act.wait_ge(norm_ok, 1)
            for b in range(4):
                norm(b, b)
            for q in range(XQ):
                if q > 0:
                    act.wait_ge(norm_ok, q + 1)
                with act.Fori(max(q * IQ, 1), (q + 1) * IQ) as i:
                    for b in range(4):
                        wait_reg(act, "act", tr_ok, 4 * i + b - 1)
                        norm(4 * i + b, b)
                        evacuate(4 * i + b - 4, b, i - 1)
                if q + 2 < XQ:
                    deviations(q + 2)
            for b in range(4):
                evacuate(T - 4 + b, b, T // 4 - 1)

            def renorm(t, b):
                return nc.scalar.activation(o_buf[:, b, :], x_tile[:, b, :], ACT.Relu, scale=rstd[:, bass.ds(t, 1)],
                                            bias=nmr[:, bass.ds(t, 1)])

            def copy_again(b):
                return nc.scalar.activation(ht_in[:, b, :], p_tr[b][:, :], ACT.Copy)

            def norm_again(t, b, i):
                wait_reg(act, "act", x_ld[b], 16 * i + 16)
                wait_reg(act, "act", o_st[b], 16 * i + 16)
                renorm(t, b).then_inc(again_ok, 1)

            def keep_again(t, b):
                wait_reg(act, "act", again_tr, t + 1)
                wait_reg(act, "act", o_ok, t + 1)
                copy_again(b).then_inc(ht_in_ok, 1)

            def score_edges(t, b):
                wait_reg(act, "act", v_ok, t + 1)
                s0 = score0[:, b, :].rearrange("p (s h) -> p s h", h=H)
                for h in range(H):
                    last = nc.scalar.activation(s0[:, :, h], vlist[:, b, :].bitcast(F32), ACT.Identity,
                                                scale=we_row[:, h:h + 1], bias=s_src[:, t, h:h + 1])
                last.then_inc(score0_ok, 1)

            def exps(t, b):
                wait_reg(act, "act", z_ok, t + 1)
                wait_reg(act, "act", sum_ok, NG * t + 2 * NG)
                nc.scalar.activation(cells[:, b * SHORT * H:(b + 1) * SHORT * H, D], z[:, 0:SHORT * H], ACT.Exp, scale=-1.0)
                nc.scalar.activation(cells[:, 2 * SHORT * H:, D], z[:, SHORT * H:], ACT.Exp, scale=-1.0).then_inc(p_ok, 1)
                act.drain()
                for s in range(SHORT - SHARE, SHORT):
                    for a in range(row(b, s) * H, row(b, s) * H + H):
                        last = nc.scalar.activation(cells[:, a, 0:D], cells[:, a, 0:D], ACT.Copy, scale=cells[:, a, D:E])
                    if (s + 1) % STEP == 0:
                        last.then_inc(a_ok, 1)

            act.wait_ge(src_ok, 1)
            act.wait_ge(consts, 3)
            count(1, 1, loaded(1, 0))
            score_edges(0, 0)
            with act.Fori(0, T // 2 - 1) as i:
                for b in range(2):
                    count(2 * i + b + 2, b, loaded(b, i + 1))
                    norm_again(2 * i + b, b, i)
                    score_edges(2 * i + b + 1, 1 - b)
                    keep_again(2 * i + b, b)
                    exps(2 * i + b, b)
            norm_again(T - 2, 0, T // 2 - 1)
            score_edges(T - 1, 1)
            keep_again(T - 2, 0)
            exps(T - 2, 0)
            norm_again(T - 1, 1, T // 2 - 1)
            keep_again(T - 1, 1)
            exps(T - 1, 1)

            act.wait_ge(todo_ok, 1)
            flagged = act.value_load(total[0:1, 0:1], min_val=0, max_val=T)
            with act.If(flagged > 0):
                with act.Fori(0, T) as t:
                    flag = act.value_load(todo[0:1, t, 0:1], min_val=0, max_val=1)
                    nth = act.value_load(todo[0:1, t, 1:2], min_val=0, max_val=T)
                    with act.If(flag > 0):
                        wait_reg(act, "act", sl_x, 16 * nth + 16)
                        renorm(t, 0).then_inc(sl_again, 1)
                        wait_reg(act, "act", sl_tr, nth + 1)
                        copy_again(0).then_inc(sl_ht, 1)
                        with act.Fori(0, NCH) as i:
                            wait_reg(act, "act", sl_z, nth * NCH + i + 1)
                            nc.scalar.activation(cells[:, 0:CHUNK * H, D], score0[:, 0, :], ACT.Exp)
                            nc.scalar.activation(corr[:, :], dmax[:, :], ACT.Exp).then_inc(sl_p, 1)

        @block.tensor
        def _(pe):
            def turn(t):
                wait_reg(pe, "pe", kept_ok, t + 3)
                nc.tensor.transpose(p_st[0:1, 0:P], kept[:, 0:1], ident[:, :])
                nc.tensor.transpose(p_st[0:1, P:2 * P], kept[:, 1:2], ident[:, :]).then_inc(worst_tr, 1)

            pe.wait_ge(consts, 2)
            pe.wait_ge(w_in, 16 * (5 + 2 * KC))
            n = 0
            for nat in (w_nat, wr_nat):
                for c in range(KC):
                    for k in range(KC):
                        if n >= 2:
                            pe.wait_ge(wtr_used, n - 1)
                        nc.tensor.transpose(p_tr[n % 2][:, 0:P], nat[:, c, k * P:(k + 1) * P],
                                            ident[:, :]).then_inc(wtr_ok, 1)
                        n += 1
            pe.wait_ge(diag_ok, 1)
            for k in range(KC):
                for c in range(KC):
                    last = nc.tensor.matmul(p_b[k][:, 0:2 * H], w_nat[:, c, k * P:(k + 1) * P], a_diag[:, c, :],
                                            start=(c == 0), stop=(c == KC - 1))
                last.then_inc(wtr_ok, 1)
            pe.wait_ge(wtr_used, n + KC)

            def tr(t, b):
                wait_reg(pe, "pe", hn_ok, t + 1)
                wait_reg(pe, "pe", ht_ok, t + 1)
                for k in range(KC):
                    last = nc.tensor.transpose(p_tr[b % 2][:, k * P:(k + 1) * P], hn[:, b, k * P:(k + 1) * P], ident[:, :])
                last.then_inc(tr_ok, 1)

            def project(t, b):
                wait_reg(pe, "pe", ht_ok, t + 3)
                wait_reg(pe, "pe", hrow_ok, t + 1)
                for k in range(KC):
                    last = nc.tensor.matmul(p_a[b % 2][:, :], h_t[:, b, k * P:(k + 1) * P], w_t[:, k, :],
                                            start=(k == 0), stop=(k == KC - 1))
                last.then_inc(mm_ok, 1)

            tr(0, 0)
            with pe.Fori(0, T // 4 - 1) as i:
                for b in range(4):
                    tr(4 * i + b + 1, (b + 1) % 4)
                    project(4 * i + b, b)
            for b in range(4):
                if b < 3:
                    tr(T - 3 + b, (b + 1) % 4)
                project(T - 4 + b, b)
            turn(0)

            def part(t, b, g, stop, n, size=GS):
                wait_reg(pe, "pe", w_ok, NG * t + g + 1)
                for s in range(g * GS + (LEAD if g == 0 else 0), g * GS + size):
                    if SHORT - SHARE <= s < SHORT and s % STEP == 0:
                        wait_reg(pe, "pe", a_ok, SHARE // STEP * t + (s - SHORT + SHARE) // STEP + 1)
                    last = nc.tensor.matmul(p_a[b][:, 0:C], ident[:, :], slots[:, row(b, s), :],
                                            start=(s == 0), stop=(stop and s == g * GS + size - 1))
                last.then_inc(sum_ok, n)

            def residual(b):
                nc.tensor.matmul(p_b[b][:, :], ident[:, :], x_tile[:, b, :], start=True, stop=False)
                for k in range(KC):
                    nc.tensor.matmul(p_b[b][:, :], ht_in[:, b, k * P:(k + 1) * P], wr_t[:, k, :],
                                     start=False, stop=False)
                return nc.tensor.matmul(p_b[b][:, :], ones[0:1, :], br_row[0:1, :], start=False, stop=True)

            def turn_again(b):
                for k in range(KC):
                    last = nc.tensor.transpose(p_tr[b][:, k * P:(k + 1) * P], o_buf[:, b, k * P:(k + 1) * P], ident[:, :])
                return last

            def sums(t, b, i):
                wait_reg(pe, "pe", again_ok, t + 1)
                turn_again(b).then_inc(again_tr, 1)
                wait_reg(pe, "pe", list_ok, t + 1)
                longest = pe.value_load(plan[0:1, b, 0:1], min_val=0, max_val=SLOTS)
                wait_reg(pe, "pe", o_ok, t + 1)
                wait_reg(pe, "pe", x_ld[b], 16 * i + 16)
                wait_reg(pe, "pe", ht_in_ok, t + 1)
                residual(b)
                wait_reg(pe, "pe", lead_ok, t + 1)
                for s in range(LEAD):
                    nc.tensor.matmul(p_a[b][:, 0:C], ident[:, :], slots[:, row(b, s), :], start=(s == 0), stop=False)
                for g in range(NS - 1):
                    part(t, b, g, False, 1)
                with pe.If(longest > SHORT):
                    part(t, b, NS - 1, False, 1)
                    with pe.If(longest > MID):
                        part(t, b, NS, True, 1)
                    with pe.Else():
                        part(t, b, NS, True, 1, MID - SHORT)
                with pe.Else():
                    part(t, b, NS - 1, True, 1 + NG - NS)

            with pe.Fori(0, T // 2 - 1) as i:
                for b in range(2):
                    turn(2 * i + b + 1)
                    sums(2 * i + b, b, i)
            turn(T - 1)
            sums(T - 2, 0, T // 2 - 1)
            sums(T - 1, 1, T // 2 - 1)

            pe.wait_ge(todo_ok, 1)
            flagged = pe.value_load(total[0:1, 0:1], min_val=0, max_val=T)
            with pe.If(flagged > 0):
                with pe.Fori(0, T) as t:
                    flag = pe.value_load(todo[0:1, t, 0:1], min_val=0, max_val=1)
                    nth = pe.value_load(todo[0:1, t, 1:2], min_val=0, max_val=T)
                    with pe.If(flag > 0):
                        wait_reg(pe, "pe", sl_x, 16 * nth + 16)
                        wait_reg(pe, "pe", sl_again, nth + 1)
                        turn_again(0).then_inc(sl_tr, 1)
                        wait_reg(pe, "pe", sl_ht, nth + 1)
                        residual(0).then_inc(sl_res, 1)
                        with pe.Fori(0, NCH) as i:
                            wait_reg(pe, "pe", sl_p, nth * NCH + i + 1)
                            wait_reg(pe, "pe", sl_w, nth * NCH + i + 1)
                            for s in range(CHUNK):
                                last = nc.tensor.matmul(p_a[0][:, 0:C], ident[:, :], slots[:, s, :],
                                                        start=(s == 0), stop=(s == CHUNK - 1))
                            last.then_inc(sl_sum, 1)

        @block.vector
        def _(v):
            V = nc.vector

            def bc(ap, shape, axis):
                return ap.unsqueeze(axis).broadcast_to(shape)

            for sm, n in ((tr_ok, 2), (ht_ok, 2), (mm_ok, 2), (hrow_ok, 2), (kept_ok, 2),
                          (o_ok, 2), (sum_ok, 2 * NG), (sl_free, 1), (sl_st, 16),
                          *((st, 16) for st in (*h_st, *o_st))):
                v.sem_inc(sm, n)
            V.memset(a_diag[:, :, :], 0.0)
            V.memset(cum[:, :, :], 0.0)
            V.memset(z[:, :], 0.0)
            v.drain()
            V.memset(z[:, 0:C].rearrange("p (h e) -> p h e", e=E)[:, :, D], PAD).then_inc(pad_ok, 1)
            V.memset(ords[:, :], 0.0)
            v.wait_ge(w_in, 16 * (5 + 2 * KC))
            v.drain()
            for n in range(2):
                for c in range(KC):
                    for q in range(HC):
                        r = slice(q * D, (q + 1) * D)
                        last = V.tensor_copy(a_diag[r, c, n * H + c * HC + q:n * H + c * HC + q + 1],
                                             a_col[r, n, c:c + 1])
            last.then_inc(diag_ok, 1)
            heads = w_t[:, :, 0:C].rearrange("p k (h e) -> p k h e", e=E)
            n = 0
            for is_r in range(2):
                for c in range(KC):
                    for k in range(KC):
                        v.wait_ge(wtr_ok, n + 1)
                        if is_r:
                            V.tensor_copy(wr_t[:, k, c * P:(c + 1) * P], p_tr[n % 2][:, 0:P]).then_inc(wtr_used, 1)
                        else:
                            V.tensor_copy(heads[:, k, c * HC:(c + 1) * HC, 0:D],
                                          p_tr[n % 2][:, 0:P].rearrange("p (h d) -> p h d", d=D)).then_inc(wtr_used, 1)
                        n += 1
            for k in range(KC):
                v.wait_ge(wtr_ok, n + k + 1)
                V.tensor_copy(w_t[:, k, C:CS], p_b[k][:, 0:H])
                V.tensor_copy(heads[:, k, :, D], p_b[k][:, H:2 * H]).then_inc(wtr_used, 1)

            v.wait_ge(base_ok, 3)
            V.tensor_scalar(seg_base[:, :], seg_i[:, :, :].rearrange("p n k -> p (n k)"), 16, None, ALU.logical_shift_left)
            V.tensor_copy(row_id[:, :], row_i[:, :])

            def f(ap):
                return ap.bitcast(F32)

            def tops(t, b, loads):
                wait_reg(v, "dve", adj_in[b], loads)
                for n in range(NSEG):
                    V.max(top_v[:, 8 * n:8 * n + 8], adj_t[:, b, n * SEG:(n + 1) * SEG])

            def columns(b):
                v.drain()
                for n in range(NSEG):
                    last = V.max_index(top_j[:, 8 * n:8 * n + 8], top_v[:, 8 * n:8 * n + 8],
                                       adj_t[:, b, n * SEG:(n + 1) * SEG])
                last.then_inc(segs_done, 1)

            def pack(t, b):
                v.drain()
                V.scalar_tensor_tensor(code[:, :], top_j[:, :], 16, seg_base[:, :], ALU.logical_shift_left, ALU.bitwise_or)
                V.tensor_scalar(junk, top_v[:, :], 0.0, 0.0, ALU.is_gt, ALU.add, accum_out=kept[:, 0:1])
                V.tensor_scalar(top_v[:, :], top_v[:, :], 0.0, None, ALU.max)
                v.drain()
                V.scalar_tensor_tensor(f(code[:, :]), top_v[:, :], 0.0, f(code[:, :]), ALU.is_gt, ALU.mult)
                v.drain()
                bits = top_v[:, :].bitcast(U32)
                V.scalar_tensor_tensor(key_lo[:, :], bits, 0xFFFF, code[:, :], ALU.bitwise_and, ALU.bitwise_or)
                V.scalar_tensor_tensor(key_hi[:, :], bits, 16, code[:, :], ALU.logical_shift_right, ALU.bitwise_or)
                v.drain()
                def largest(r, extra=()):
                    s = slice(8 * r, 8 * r + 8)
                    for lst, key in ((list_hi, key_hi), (list_lo, key_lo)):
                        V.max(f(lst[:, s]), f(key[:, :]))
                    for step in extra:
                        step()

                def strike(r, extra=()):
                    s = slice(8 * r, 8 * r + 8)
                    for lst, key in ((list_hi, key_hi), (list_lo, key_lo)):
                        V.match_replace(f(key[:, :]), f(lst[:, s]), f(key[:, :]), 0.0)
                    for step in extra:
                        step()

                def rank(r, between=(), after=()):
                    largest(r, between)
                    v.drain()
                    strike(r, after)
                    v.drain()

                def counted_row():
                    wait_reg(v, "dve", count_ok, t + 1)
                    V.tensor_reduce(kept[:, 1:2], npos[:, b, :], axis=AX.X, op=ALU.add)

                def lost():
                    V.tensor_tensor(kept[:, 1:2], kept[:, 1:2], kept[:, 0:1], ALU.not_equal)

                def flag_row():
                    V.scalar_tensor_tensor(kept[:, 1:2], kept[:, 0:1], float(SLOTS), kept[:, 1:2],
                                           ALU.is_gt, ALU.max).then_inc(kept_ok, 1)

                def longest_row():
                    wait_reg(v, "dve", worst_tr, t + 1)
                    V.tensor_reduce(worst[:, :], p_st[0:1, :].rearrange("p (a q) -> p a q", q=P), axis=AX.X, op=ALU.max)

                def flag_tile():
                    V.tensor_copy(flags[0:1, bass.ds(t, 1)], worst[:, 1:2])
                    V.tensor_scalar(cut[:, 0:1], worst[:, 0:1], float(SLOTS), None, ALU.min)

                def parts_over():
                    for n, g in enumerate((NS - 1, NS)):
                        V.tensor_scalar(cut[:, n + 1:n + 2], cut[:, 0:1], float(-GS * g),
                                        FIRM % GS if n == 0 else 0.0, ALU.add, ALU.max)

                def parts_count():
                    V.tensor_scalar(cut[:, 1:], cut[:, 1:], float(GS), 16.0, ALU.min, ALU.mult)

                def counted():
                    V.tensor_tensor(cum[:, b, 1:], cum[:, b, 1:], cut[:, 1:], ALU.add)
                    V.tensor_copy(cum[:, b, 0:1], cut[:, 0:1])

                def make_plan():
                    V.tensor_copy(plan[:, b, :], cum[:, b, :]).then_inc(plan_self, 1)

                rank(0, (counted_row,), (lost,))
                rank(1, (flag_row,))
                rank(2, (), (longest_row,))
                rank(3, (flag_tile,), (parts_over,))
                rank(4, (parts_count,), (counted,))
                make_plan()
                last = SHORT // 8 - 1
                largest(last)
                wait_reg(v, "dve", plan_self, t + 1)
                longest = v.value_load(plan[0:1, b, 0:1], min_val=0, max_val=SLOTS)
                v.drain()
                with v.If(longest > SHORT):
                    strike(last)
                    v.drain()
                    largest(last + 1)
                    with v.If(longest > MID):
                        v.drain()
                        strike(last + 1)
                        v.drain()
                        largest(last + 2)
                    with v.Else():
                        V.memset(list_hi[:, MID:], 0)
                        V.memset(list_lo[:, MID:], 0)
                with v.Else():
                    V.memset(list_hi[:, SHORT:], 0)
                    V.memset(list_lo[:, SHORT:], 0)
                v.drain()
                V.tensor_scalar(vhi, list_hi[:, :], 0xFFFF, 16, ALU.bitwise_and, ALU.logical_shift_left)
                V.tensor_scalar(nb, list_hi[:, :], 16, CODE - 1, ALU.logical_shift_right, ALU.bitwise_and)
                V.tensor_scalar(own, f(list_hi[:, :]), 0.0, row_id[:, 0:1], ALU.is_equal, ALU.mult)
                V.tensor_scalar(pen[:, b, FIRM:], f(list_hi[:, FIRM:]), 0.0, PAD, ALU.is_equal, ALU.mult)
                v.drain()
                V.scalar_tensor_tensor(vlist[:, b, :], list_lo[:, :], 0xFFFF, vhi,
                                       ALU.bitwise_and, ALU.bitwise_or).then_inc(v_ok, 1)
                V.tensor_tensor(idx[:, b, :], nb, own, ALU.add).then_inc(list_ok, 1)

            def stats_of(t):
                for k in range(4):
                    V.bn_stats(stats[:, t + k, :], x_sb[:, t + k, :])

            def moments(q):
                r = slice(q * TQ, (q + 1) * TQ)
                v.drain()
                V.tensor_tensor(mom[:, 0, r], stats[:, r, 1], stats[:, r, 4], ALU.add)
                V.tensor_tensor(mom[:, 1, r], stats[:, r, 2], stats[:, r, 5], ALU.add)
                V.tensor_tensor(mom[:, 2, r], stats[:, r, 1], stats[:, r, 4], ALU.subtract)
                v.drain()
                V.tensor_tensor(mom[:, 2, r], mom[:, 2, r], mom[:, 2, r], ALU.mult)
                V.tensor_scalar(mom[:, 0, r], mom[:, 0, r], 0.5, None, ALU.mult)
                V.tensor_scalar(mom[:, 1, r], mom[:, 1, r], 1.0 / IN, EPS, ALU.mult, ALU.add)
                v.drain()
                V.scalar_tensor_tensor(mom[:, 1, r], mom[:, 2, r], 0.25, mom[:, 1, r],
                                       ALU.mult, ALU.add).then_inc(var_ok, 1)
                v.wait_ge(std_ok, q + 1)
                V.reciprocal(rstd[:, r], rstd[:, r])
                v.drain()
                V.scalar_tensor_tensor(nmr[:, r], mom[:, 0, r], -1.0, rstd[:, r], ALU.mult, ALU.mult).then_inc(norm_ok, 1)

            v.drain()
            for q in range(2):
                v.wait_ge(x_in[q], 16)
                with v.Fori(q * IQ, (q + 1) * IQ) as i:
                    stats_of(4 * i)
                moments(q)

            def copy_ht(i, b):
                wait_reg(v, "dve", tr_ok, 4 * i + b + 3)
                V.tensor_copy(h_t[:, b, :], p_tr[b % 2][:, :]).then_inc(ht_ok, 1)

            for q in range(XQ // 2):
                v.wait_ge(x_in[q + 2], 16)
                with v.Fori(q * IQ, (q + 1) * IQ) as i:
                    for b in range(4):
                        copy_ht(i, b)
                        t = 4 * i + b + 2 * TQ
                        V.bn_stats(stats[:, t, :], x_sb[:, t, :])
                moments(q + 2)
            v.wait_ge(adj_in[0], loaded(0, 0))
            v.wait_ge(pad_st, 16)
            for i in range(2 * IQ, 4 * IQ):
                if i == 3 * IQ:
                    v.drain()
                for b in range(4):
                    copy_ht(i, b)
                    for k in range(SEG_I // 4):
                        n = (i % IQ) * SEG_I + b * SEG_I // 4 + k
                        top, seg = slice(8 * n, 8 * n + 8), slice(SEG * n, SEG * n + SEG)
                        if i < 3 * IQ:
                            V.max(top_v[:, top], adj_t[:, 0, seg])
                        else:
                            V.max_index(top_j[:, top], top_v[:, top], adj_t[:, 0, seg])
                    if b % 2 == 1:
                        n = (i - 2 * IQ) * 2 + b // 2
                        v.drain()
                        V.tensor_scalar(z[:, :], adj_t[:, 0, n * CNT:(n + 1) * CNT], 0.0, 0.0,
                                        ALU.is_gt, ALU.add, accum_out=npos[:, 0, n:n + 1])
            v.drain().then_inc(count_ok, 1)
            v.drain().then_inc(segs_done, 1)
            pack(0, 0)

            def score(t, b, n):
                zz = z[:, 0:n * H]
                z3 = zz.rearrange("p (s h) -> p s h", h=H)
                for s0, s1 in ((0, SHORT), (SHORT, n))[:1 + (n > SHORT)]:
                    V.tensor_tensor(z[:, s0 * H:s1 * H], score0[:, b, s0 * H:s1 * H],
                                    cells[:, row(b, s0) * H:row(b, s1 - 1) * H + H, D], ALU.add)
                v.drain()
                V.tensor_tensor(z3[:, FIRM:, :], z3[:, FIRM:, :], bc(pen[:, b, FIRM:n], [P, n - FIRM, H], 2), ALU.add)
                v.drain()
                V.scalar_tensor_tensor(zz, zz, ALPHA, zz, ALU.mult, ALU.max)
                v.drain()
                V.tensor_reduce(gmax[:, :], zz.rearrange("p (s h) -> p h s", h=H), axis=AX.X, op=ALU.max)
                v.drain()
                V.scalar_tensor_tensor(z3, bc(gmax[:, :], [P, n, H], 1), FLOOR, z3, ALU.max, ALU.subtract).then_inc(z_ok, 1)

            def weigh(b, s, n, done, by=1):
                a = slice(row(b, s) * H, row(b, s) * H + n * H)
                V.tensor_tensor(cells[:, a, 0:D], cells[:, a, 0:D],
                                cells[:, a, D:E].broadcast_to([P, n * H, D]), ALU.mult).then_inc(done, by)

            def planned(b):
                return [v.value_load(plan[0:1, b, n:n + 1], min_val=lo, max_val=hi) for n, lo, hi in
                        ((0, 0, SLOTS), (1, 16, 16 * GS * T), (2, 0, 16 * GS * T))]

            def attend(t, b, i, prev, regs):
                longest, upto_a, upto_b = regs
                wait_reg(v, "dve", score0_ok, t + 1)
                for g in range(NS - 1):
                    wait_reg(v, "dve", rows_in[b][g], (i + 1) * 16 * GS)
                wait_reg(v, "dve", rows_in[b][NS - 1], upto_a)
                with v.If(longest > SHORT):
                    wait_reg(v, "dve", rows_in[b][NS], upto_b)
                    with v.If(longest > MID):
                        score(t, b, SLOTS)
                    with v.Else():
                        score(t, b, MID)
                with v.Else():
                    score(t, b, SHORT)
                if prev is not None:
                    settle(*prev)
                wait_reg(v, "dve", p_ok, t + 1)
                weigh(b, 0, LEAD, lead_ok)
                weigh(b, LEAD, GS - LEAD, w_ok)
                for g in range(1, NS - 1):
                    weigh(b, g * GS, GS, w_ok)
                with v.If(longest > SHORT):
                    weigh(b, SHORT - GS, GS - SHARE, w_ok)
                    with v.If(longest > MID):
                        weigh(b, SHORT, SLOTS - SHORT, w_ok)
                    with v.Else():
                        weigh(b, SHORT, MID - SHORT, w_ok)
                with v.Else():
                    weigh(b, SHORT - GS, GS - SHARE, w_ok, 1 + NG - NS)

            def settle(t, b, i):
                wait_reg(v, "dve", sum_ok, NG * t + 3 * NG)
                wait_reg(v, "dve", o_st[b], 16 * i + 16)
                finish(b, p_a[b][:, 0:C], o_ok)

            def finish(b, sums, ready):
                a3 = sums.rearrange("p (h e) -> p h e", e=E)
                V.reciprocal(rden[:, :], a3[:, :, D])
                v.drain()
                V.tensor_tensor(o_buf[:, b, :].rearrange("p (h d) -> p h d", d=D), a3[:, :, 0:D],
                                bc(rden[:, :], [P, H, D], 2), ALU.mult)
                v.drain()
                V.tensor_tensor(o_buf[:, b, :], o_buf[:, b, :], p_b[b][:, :], ALU.add).then_inc(ready, 1)

            v.wait_ge(hrow_ok, T + 2)
            V.tensor_tensor(s_src[:, :, :], s_src[:, :, :], bc(be_row[:, :], [P, T, H], 1), ALU.add).then_inc(src_ok, 1)
            v.wait_ge(consts, 3)
            tops(1, 1, loaded(1, 0))
            columns(1)
            regs = planned(0)
            pack(1, 1)
            tops(2, 0, loaded(0, 1))
            attend(0, 0, 0, None, regs)
            with v.Fori(0, T // 2 - 2) as i:
                regs = planned(1)
                columns(0)
                pack(2 * i + 2, 0)
                tops(2 * i + 3, 1, loaded(1, i + 1))
                attend(2 * i + 1, 1, i, (2 * i, 0, i), regs)
                regs = planned(0)
                columns(1)
                pack(2 * i + 3, 1)
                tops(2 * i + 4, 0, loaded(0, i + 2))
                attend(2 * i + 2, 0, i + 1, (2 * i + 1, 1, i), regs)
            i = T // 2 - 2
            regs = planned(1)
            columns(0)
            pack(T - 2, 0)
            tops(T - 1, 1, loaded(1, i + 1))
            attend(T - 3, 1, i, (T - 4, 0, i), regs)
            regs = planned(0)
            columns(1)
            pack(T - 1, 1)
            attend(T - 2, 0, i + 1, (T - 3, 1, i), regs)
            attend(T - 1, 1, i + 1, (T - 2, 0, i + 1), planned(1))
            settle(T - 1, 1, T // 2 - 1)

            v.drain()
            V.tensor_tensor_scan(ords[0:1, 1:], flags[0:1, :], flags[0:1, :], 0.0, ALU.add, ALU.bypass)
            V.tensor_copy(todo[0:1, :, 0], flags[0:1, :])
            v.drain()
            V.tensor_copy(total[0:1, :], ords[0:1, T:])
            v.drain()
            V.tensor_copy(todo[0:1, :, 1], ords[0:1, 0:T]).then_inc(todo_ok, 1)
            v.wait_ge(todo_ok, 1)
            flagged = v.value_load(total[0:1, 0:1], min_val=0, max_val=T)
            with v.If(flagged > 0):
                with v.Fori(0, T) as t:
                    flag = v.value_load(todo[0:1, t, 0:1], min_val=0, max_val=1)
                    nth = v.value_load(todo[0:1, t, 1:2], min_val=0, max_val=T)
                    with v.If(flag > 0):
                        V.memset(m[:, 0, :], FLOOR)
                        V.memset(acc, 0.0)
                        with v.Fori(0, NCH) as i:
                            n = nth * NCH + i
                            s3 = [P, CHUNK, H]
                            s0 = score0[:, 0, :].rearrange("p (s h) -> p s h", h=H)
                            a3 = acc.rearrange("p (h e) -> p h e", e=E)
                            wait_reg(v, "dve", sl_v, 16 * n + 16)
                            V.tensor_tensor(s0, bc(v_in, s3, 2), bc(we_row[:, :], s3, 1), ALU.mult)
                            V.tensor_scalar(pen[:, 0, :], v_in, 0.0, PAD, ALU.is_le, ALU.mult)
                            v.drain()
                            V.tensor_tensor(s0, s0, s_src[:, bass.ds(t, 1), :].broadcast_to(s3), ALU.add)
                            wait_reg(v, "dve", sl_h, 16 * n + 16)
                            v.drain()
                            V.tensor_tensor(score0[:, 0, :], score0[:, 0, :], cells[:, 0:CHUNK * H, D], ALU.add)
                            v.drain()
                            V.tensor_tensor(s0, s0, bc(pen[:, 0, :], s3, 2), ALU.add)
                            v.drain()
                            V.scalar_tensor_tensor(s0, s0, ALPHA, s0, ALU.mult, ALU.max)
                            v.drain()
                            V.tensor_reduce(gmax[:, :], s0.rearrange("p s h -> p h s"), axis=AX.X, op=ALU.max)
                            v.drain()
                            V.tensor_tensor(m[:, 1, :], gmax[:, :], m[:, 0, :], ALU.max)
                            v.drain()
                            V.tensor_tensor(dmax[:, :], m[:, 0, :], m[:, 1, :], ALU.subtract)
                            v.drain()
                            V.tensor_copy(m[:, 0, :], m[:, 1, :])
                            V.tensor_tensor(s0, s0, bc(m[:, 1, :], s3, 1), ALU.subtract).then_inc(sl_z, 1)
                            wait_reg(v, "dve", sl_p, n + 1)
                            V.tensor_tensor(cells[:, 0:CHUNK * H, 0:D], cells[:, 0:CHUNK * H, 0:D],
                                            cells[:, 0:CHUNK * H, D:E].broadcast_to([P, CHUNK * H, D]), ALU.mult).then_inc(sl_w, 1)
                            V.tensor_tensor(a3, a3, bc(corr[:, :], [P, H, E], 2), ALU.mult)
                            wait_reg(v, "dve", sl_sum, n + 1)
                            v.drain()
                            V.tensor_tensor(acc, acc, p_a[0][:, 0:C], ALU.add).then_inc(sl_free, 1)
                        v.drain()
                        wait_reg(v, "dve", sl_res, nth + 1)
                        wait_reg(v, "dve", sl_st, 16 * nth + 16)
                        finish(0, acc, sl_o)
                        v.drain()


_INS = ["x", "adj", "L0_gnn_W", "L0_gnn_We", "L0_gnn_be", "L0_gnn_a_src", "L0_gnn_a_dst", "L0_gnn_Wr", "L0_gnn_br"]


def kernel(**inputs):
    import numpy as _np
    import concourse.bacc as _bacc
    from concourse import mybir as _mybir
    from concourse.bass_utils import run_bass_kernel_spmd as _run

    nc = _bacc.Bacc("TRN2", target_bir_lowering=False, num_devices=1)
    arrays, args = {}, []
    for name in _INS:
        a = _np.ascontiguousarray(inputs[name])
        arrays[f"in_{name}_dram"] = a
        args.append(nc.dram_tensor(f"in_{name}_dram", a.shape, _mybir.dt.from_np(a.dtype), kind="ExternalInput").ap())
    args.append(nc.dram_tensor("out_0_dram", inputs["x"].shape, _mybir.dt.float32, kind="ExternalOutput").ap())
    build(nc, *args)
    r = _run(nc, [arrays], core_ids=[0])
    return r.results[0]["out_0_dram"]
```
